# Optimizing a Trainium2 kernel written in Bass

```python
import numpy as np
import jax
import jax.numpy as jnp

def _softmax(x, axis=-1):
    return jax.nn.softmax(x, axis=axis)

def _gelu(x):
    return jax.nn.gelu(x, approximate=True)

def _silu(x):
    return jax.nn.silu(x)

def _sigmoid(x):
    return jax.nn.sigmoid(x)

def _layernorm(x, axis=-1, eps=1e-05):
    m = jnp.mean(x, axis=axis, keepdims=True)
    v = jnp.var(x, axis=axis, keepdims=True)
    return (x - m) / jnp.sqrt(v + eps)

def _scatter_add(tgt, idx, src, axis=0):
    return tgt.at[idx].add(src)

def _segment_sum(src, seg, n):
    return jax.ops.segment_sum(src, seg, n)
kernel_name = 'mk_gnn_preln_d1_gnn_r32_6acc6c'

def setup_inputs(seed: int=0):
    np.random.seed(seed)
    _w = jnp.asarray

    def _rec_inputs():
        import jax
        import jax.numpy as jnp
        _gk = jax.random.key(seed)
        x = -0.0002117 + 1 * jax.random.normal(jax.random.fold_in(_gk, 1), (3125, 256), jnp.float32)
        src = jax.random.randint(jax.random.fold_in(_gk, 2), (50000,), 0, 3125, jnp.int32)
        dst = jax.random.randint(jax.random.fold_in(_gk, 3), (50000,), 0, 3125, jnp.int32)
        _o = jnp.argsort(dst, stable=True)
        src = src[_o]
        dst = dst[_o]
        return (x, src, dst)
    x, src, dst = _rec_inputs()

    def _L0_gnn_setup():
        import jax, jax.numpy as jnp
        import numpy as np
        N_NODES = 3125
        N_EDGES = 10000
        D_IN, D_HID, D_OUT = (256, 1024, 256)
        BN_EPS = 1e-05
        key = jax.random.key(seed)
        ks = jax.random.split(key, 6)
        x = jax.random.normal(ks[0], (N_NODES, D_IN), dtype=jnp.float32)
        edge_index = jax.random.randint(ks[1], (2, N_EDGES), 0, N_NODES, dtype=jnp.int64)
        W1 = jax.random.normal(ks[2], (D_IN, D_HID), dtype=jnp.float32) * (1.0 / np.sqrt(D_IN))
        b1 = jnp.zeros((D_HID,), dtype=jnp.float32)
        gamma = jnp.ones((D_HID,), dtype=jnp.float32)
        beta = jnp.zeros((D_HID,), dtype=jnp.float32)
        W2 = jax.random.normal(ks[3], (D_HID, D_OUT), dtype=jnp.float32) * (1.0 / np.sqrt(D_HID))
        b2 = jnp.zeros((D_OUT,), dtype=jnp.float32)
        return {'x': x, 'edge_index': edge_index, 'W1': W1, 'b1': b1, 'gamma': gamma, 'beta': beta, 'W2': W2, 'b2': b2}
    _L0_gnn_all = _L0_gnn_setup()
    _L0_gnn_in = {k: v for k, v in _L0_gnn_all.items() if k in ('W1', 'b1', 'gamma', 'beta', 'W2', 'b2')}
    del _L0_gnn_all
    return {'x': x, 'src': src, 'dst': dst, 'L0_gnn_W1': _L0_gnn_in['W1'], 'L0_gnn_b1': _L0_gnn_in['b1'], 'L0_gnn_gamma': _L0_gnn_in['gamma'], 'L0_gnn_beta': _L0_gnn_in['beta'], 'L0_gnn_W2': _L0_gnn_in['W2'], 'L0_gnn_b2': _L0_gnn_in['b2']}

def reference(x, src, dst, L0_gnn_W1, L0_gnn_b1, L0_gnn_gamma, L0_gnn_beta, L0_gnn_W2, L0_gnn_b2):
    import jax
    import jax.numpy as jnp

    def _L0_gnn_ref(x, edge_index, W1, b1, gamma, beta, W2, b2):
        import jax, jax.numpy as jnp
        import numpy as np
        N_NODES = 3125
        N_EDGES = 10000
        D_IN, D_HID, D_OUT = (256, 1024, 256)
        BN_EPS = 1e-05
        src, dst = (edge_index[0], edge_index[1])
        agg = jax.ops.segment_sum(x[src], dst, num_segments=x.shape[0])
        h = agg + x
        h1 = h @ W1 + b1
        mean = jnp.mean(h1, axis=0)
        var = jnp.mean(jnp.square(h1 - mean), axis=0)
        h1 = (h1 - mean) * jax.lax.rsqrt(var + BN_EPS) * gamma + beta
        h1 = jax.nn.relu(h1)
        out = jax.nn.relu(h1 @ W2 + b2)
        return out
    edge_index = jnp.stack([src, dst])
    h = jnp.maximum(_layernorm(x, axis=-1), 0.0)
    x = x + _L0_gnn_ref(h, edge_index, L0_gnn_W1, L0_gnn_b1, L0_gnn_gamma, L0_gnn_beta, L0_gnn_W2, L0_gnn_b2)
    return x

_drawn_inputs = setup_inputs


def setup_inputs(seed=0):
    import zlib

    import numpy as np

    out = dict(_drawn_inputs(seed))
    spreads = {'L0_gnn_b1': (0.0, 0.1),
     'L0_gnn_gamma': (1.0, 0.2),
     'L0_gnn_beta': (0.0, 0.1),
     'L0_gnn_b2': (0.0, 0.1)}
    factors = {}
    for name, (base, spread) in spreads.items():
        noise = np.random.default_rng([zlib.crc32(name.encode()), seed]).standard_normal(out[name].shape)
        drawn = base * np.exp(spread * noise) if base else spread * noise
        out[name] = jnp.asarray(drawn.astype(out[name].dtype))
    for name, factor in factors.items():
        out[name] = (out[name] * factor).astype(out[name].dtype)
    return out
```

```python
from contextlib import ExitStack

import concourse.bass as bass
from concourse import mybir

F32 = mybir.dt.float32
BF16 = mybir.dt.bfloat16
I32 = mybir.dt.int32
ALU = mybir.AluOpType
ACT = mybir.ActivationFunctionType
AX = mybir.AxisListType

N, D, H, E = 3125, 256, 1024, 50000
EPS = 1e-5
P = 128
KD, KH = D // P, H // P

NP = 125
NT = N // NP
XT = 5
XG = NT // XT
LO = 112

CG = 4
G = -(-E // (P * CG))
C = G * CG
CT = -(-G // 4) * 4 * CG
RC = C // 4
STEP = 32
W = 112
BACK = 40
PARTS = 3
ROW = PARTS * D
HTW = BACK + STEP * (G - 1) - BACK + W

FREE = 2
Q = 4
SUP = 16
NB = 512
NSUP = G // SUP
TAIL_A = (NB * (NSUP - 1), 384)
TAIL_B = (NB * (NSUP - 1) + 384, N - NB * (NSUP - 1) - 384)
NSTAT = NSUP - 1 + 2
FIRST_HID = 2
HALF = NB // 2
REST = N - NSUP * NB
GB = -(-N // NB)


def build(nc, x, src, dst, W1, b1, gamma, beta, W2, b2, out):
    h_rows = nc.dram_tensor("h_rows", [N + 1, ROW], BF16).ap()
    ctx = ExitStack()
    with ctx:
        def sb(name, shape, dt):
            return ctx.enter_context(nc.sbuf_tensor(name, shape, dt))

        def sem(name):
            return ctx.enter_context(nc.semaphore(name))

        h1T = sb("h1T", [P, KH * N], F32)
        h1 = h1T[:, :].rearrange("p (k n) -> p k n", k=KH)
        x_sb = h1T[:, 0:NT * D].rearrange("p (t d) -> p t d", t=NT)
        h32 = h1T[:, NT * D:2 * NT * D].rearrange("p (t d) -> p t d", t=NT)
        node_iota = h1T[:, 0:N]
        onehot_all = h1T[:, N + 1:N + 1 + (N + 1) // 2].bitcast(BF16)[:, 0:N]
        at = 2 * NT * D
        hp = (h1T[0:NP, at:at + NT * PARTS * D // 2].bitcast(BF16)
              .rearrange("p (t s d) -> p t s d", t=NT, s=PARTS))
        at += NT * PARTS * D // 2
        edge_i = h1T[0:RC, at:at + 8 * P].bitcast(I32).rearrange("p (a t e) -> p a t e", a=2, t=4)
        at += 8 * P
        edge_f = h1T[0:RC, at:at + 8 * P].rearrange("p (a t e) -> p a t e", a=2, t=4)
        hT = sb("hT", [P, KD, HTW], F32)
        res = sb("res", [NP, XT, D], F32)
        w1 = sb("w1", [P, KD, H], F32)
        w2 = sb("w2", [P, KH, D], F32)
        b2b = sb("b2b", [P, D], F32)
        vec_rows = sb("vec_rows", [3 * KH, P], F32)
        vec = sb("vec", [P, 3 * KH], F32)
        ident = sb("ident", [P, P], F32)
        ones = sb("ones", [P, 1], F32)
        zrow = sb("zrow", [1, ROW], BF16)
        zcols = sb("zcols", [P, NB], BF16)
        epst = sb("epst", [P, 1], F32)
        src_tab = sb("src_tab", [P, CT], I32)
        dst_tab = sb("dst_tab", [P, C], F32)
        dst_rel = sb("dst_rel", [P, CT], F32)
        win_i = sb("win_i", [P, G, CG], I32)
        win_f = sb("win_f", [P, G, CG], F32)
        iota_i = sb("iota_i", [P, W], I32)
        iota_f = sb("iota_f", [P, W], F32)
        lim = sb("lim", [P, 4], F32)
        flag = sb("flag", [1, 1], I32)
        stats = sb("stats", [NP, NT, 6], F32)
        mv = sb("mv", [NP, NT, 2], F32)
        std = sb("std", [NP, NT], F32)
        rstd = sb("rstd", [NP, NT], F32)
        nbias = sb("nbias", [NP, NT], F32)
        idx_ring = sb("idx_ring", [P, Q, CG], I32)
        g_ring = sb("g_ring", [P, Q, CG, ROW], BF16)
        d_ring = sb("d_ring", [P, Q, CG, W], BF16)
        bst = sb("bst", [P, KH, NSTAT, 6], F32)
        bmv = sb("bmv", [P, KH, 2], F32)
        bstd = sb("bstd", [P, KH], F32)
        brstd = sb("brstd", [P, KH], F32)
        bscale = sb("bscale", [P, KH], F32)
        bms = sb("bms", [P, KH], F32)
        bshift = sb("bshift", [P, KH], F32)
        over = g_ring[:, :, :, :].rearrange("p q c r -> p (q c r)").bitcast(F32)
        hn = over[:, 0:2 * KH * HALF].rearrange("p (b k n) -> p b k n", b=2, k=KH)
        o2 = over[:, 2 * KH * HALF:2 * KH * HALF + 4 * D].rearrange("p (b s d) -> p b s d", b=2, s=2)
        x2 = sb("x2", [P, 2, 2, D], F32)

        ps = ctx.enter_context(nc.psum_tensor("ps", [P, 8, NB], F32))
        p_win = [ps[:, b, 0:KD * W].rearrange("p (f w) -> p f w", f=KD) for b in (0, 1)]
        p_hid = [ps[:, b, :] for b in (2, 3)]
        p_tr = [ps[:, b, 0:KD * NP].rearrange("p (f n) -> p f n", f=KD) for b in (4, 5)]
        p_tab = [ps[:, b, 0:C] for b in (6, 7)]
        p_out = [ps[:, b, :].rearrange("p (s d) -> p s d", s=2) for b in (4, 5)]

        s_x = [sem(f"x_loaded{g}") for g in range(XG)]
        s_edges = sem("edges_loaded")
        s_vecs = sem("vecs_loaded")
        s_w1 = sem("w1_loaded")
        s_w2 = sem("w2_loaded")
        s_b2 = sem("b2_loaded")
        s_hrow = sem("h_rows_stored")
        s_const = sem("consts_made")
        s_pads = sem("pads_made")
        s_ident = sem("ident_made")
        s_efl = sem("edges_as_float")
        s_tabT = sem("tables_transposed")
        s_tab = sem("tables_ready")
        s_viol = sem("violations_known")
        s_vsum = sem("violations_summed")
        s_flag = sem("flag_ready")
        s_vecT = sem("vecs_transposed")
        s_vec = sem("vecs_ready")
        s_var = sem("variances_ready")
        s_std = sem("stds_ready")
        s_norm = sem("norms_ready")
        s_h32 = sem("h_made")
        s_hi = sem("hi_made")
        s_res = sem("residue_made")
        s_mid = sem("mid_made")
        s_lo = sem("lo_made")
        s_hTp = sem("h_transposed")
        s_hTc = sem("hT_copied")
        s_pad = sem("hT_pads_zero")
        s_dve = sem("dve_step")
        s_idx = sem("indices_ready")
        s_turn = sem("pool_turn")
        s_gath = [sem(f"gathered{q}") for q in range(Q)]
        s_hot = sem("onehots_ready")
        s_win = sem("window_summed")
        s_add = sem("window_added")
        s_hid = sem("hidden_computed")
        s_h1 = sem("hidden_stored")
        s_bst = sem("hidden_stats")
        s_gidx = sem("general_index_ready")
        s_ggath = sem("general_gathered")
        s_ghot = sem("general_onehot_ready")
        s_giota = sem("general_iota_ready")
        s_gused = sem("general_chunk_used")
        s_gopen = sem("general_sums_closed")
        s_gadd = sem("general_added")
        s_bvar = sem("bn_var_ready")
        s_bsd = sem("bn_std_ready")
        s_bn = sem("bn_ready")
        s_hn = sem("normalised")
        s_out = sem("outputs_computed")
        s_x2 = [sem(f"residual_loaded{b}") for b in (0, 1)]
        s_bias = sem("bias_added")
        s_o2 = sem("outputs_ready")
        s_st = [sem(f"stored{b}") for b in (0, 1)]

        block = ctx.enter_context(nc.Block())

        def x_view(dram, g):
            rows = dram[g * XT * NP:(g + 1) * XT * NP, :]
            return rows.rearrange("(t p) d -> p t d", p=NP)

        def tail_rows(dram):
            return dram[NSUP * NB:N, :]

        @block.sync
        def _(sp):
            for g in range(XG):
                v = x_view(x, g)
                for a, b in ((0, LO), (LO, NP)):
                    sp.dma_start(x_sb[a:b, g * XT:(g + 1) * XT, :], v[a:b]).then_inc(s_x[g], 16)
            for g in range(XG):
                sp.wait_ge(s_lo, g + 1)
                v = x_view(h_rows, g)
                for a, b in ((0, LO), (LO, NP)):
                    sp.dma_start(v[a:b], hp[a:b, g * XT:(g + 1) * XT, :, :]
                                 .rearrange("p t s d -> p t (s d)")).then_inc(s_hrow, 16)
            sp.dma_start(w2[:, :, :], W2.rearrange("(k p) d -> p k d", p=P)).then_inc(s_w2, 16)
            sp.dma_start(b2b[:, :], b2.rearrange("(a d) -> a d", a=1).to_broadcast([P, D])).then_inc(s_b2, 16)

            def load(row0, b):
                sp.dma_start(x2[:, b, :, :],
                             x[bass.ds(row0, HALF), :].rearrange("(s p) d -> p s d", p=P)).then_inc(s_x2[b], 16)

            def store(row0, b):
                sp.dma_start(out[bass.ds(row0, HALF), :].rearrange("(s p) d -> p s d", p=P),
                             o2[:, b, :, :]).then_inc(s_st[b], 16)

            for b in (0, 1):
                load(b * HALF, b)
            with sp.Fori(0, NSUP - 1) as i:
                for b in (0, 1):
                    sp.wait_ge(s_o2, 2 * i + b + 1)
                    store(i * NB + b * HALF, b)
                    load((i + 1) * NB + b * HALF, b)
            for b in (0, 1):
                sp.wait_ge(s_o2, 2 * (NSUP - 1) + b + 1)
                store((NSUP - 1) * NB + b * HALF, b)
                if b == 0:
                    sp.dma_start(x2[0:REST, 0, 0, :], tail_rows(x)).then_inc(s_x2[0], 16)
            sp.wait_ge(s_o2, 2 * NSUP + 1)
            sp.dma_start(tail_rows(out), o2[0:REST, 0, 0, :]).then_inc(s_st[0], 16)
            sp.wait_ge(s_st[0], 16 * (NSUP + 1))
            sp.wait_ge(s_st[1], 16 * NSUP)

        @block.gpsimd
        def _(pool):
            pool.memset(edge_i[RC - 2:RC, 0, 3, :], N).then_inc(s_pads, 1)
            pool.wait_ge(s_pads, 1)
            pool.memset(edge_i[RC - 2:RC, 1, 3, :], N - 1).then_inc(s_pads, 1)
            pool.wait_ge(s_pads, 2)
            pool.memset(ident[:, :], 0.0).then_inc(s_ident, 1)
            pool.memset(zrow[:, :], 0.0).then_inc(s_const, 1)
            pool.memset(ones[:, :], 1.0).then_inc(s_const, 1)
            pool.memset(epst[:, :], EPS).then_inc(s_const, 1)
            pool.iota(iota_i[:, :], pattern=[[1, W]], base=0, channel_multiplier=0).then_inc(s_const, 1)
            pool.iota(win_i[:, :, :], pattern=[[STEP, G], [0, CG]], base=-BACK,
                      channel_multiplier=0).then_inc(s_const, 1)
            pool.wait_ge(s_ident, 1)
            pool.affine_select(out=ident[:, :], in_=ident[:, :], compare_op=ALU.not_equal, fill=1.0, base=0,
                               pattern=[[-1, P]], channel_multiplier=1).then_inc(s_ident, 1)
            pool.memset(hT[:, :, 0:BACK], 0.0).then_inc(s_pad, 1)
            pool.memset(hT[:, :, BACK + N:HTW], 0.0).then_inc(s_pad, 1)
            pool.memset(zcols[:, :], 0.0).then_inc(s_pad, 1)
            pool.memset(src_tab[:, C:CT], 0).then_inc(s_pad, 1)
            pool.memset(dst_rel[:, C:CT], -1.0).then_inc(s_pad, 1)

            pool.wait_ge(s_flag, 1)
            irregular = pool.value_load(flag[0:1, 0:1], min_val=0, max_val=1)
            pool.wait_ge(s_hrow, 16 * (2 * XG + 1))

            def gather(to, index, done):
                pool.indirect_dma_start(to, None, h_rows,
                                        bass.IndirectOffsetOnAxis(ap=index, axis=0)).then_inc(done, 16)

            with pool.If(irregular == 0):
                def group(q, g, first):
                    pool.wait_ge(s_idx, g + 1)
                    if not first:
                        pool.wait_ge(s_win, g - Q + 1)
                    pool.sem_inc(s_turn, 1)
                    for c in range(CG):
                        gather(g_ring[:, q, c, :], idx_ring[:, q, c:c + 1], s_gath[q])

                for q in range(Q):
                    group(q, q, True)
                with pool.Fori(1, G // Q) as r:
                    for q in range(Q):
                        group(q, r * Q + q, False)
                for g in range(G // Q * Q, G):
                    group(g % Q, g, False)
            with pool.Else():
                pool.iota(node_iota.bitcast(I32), pattern=[[1, N]], base=0,
                          channel_multiplier=0).then_inc(s_giota, 1)
                with pool.Fori(0, KD * C) as c:
                    pool.wait_ge(s_gidx, c + 1)
                    pool.sem_inc(s_turn, 1)
                    gather(g_ring[:, 0, 0, :], idx_ring[:, 0, 0:1], s_ggath)

        @block.tensor
        def _(pe):
            pe.wait_ge(s_ident, 2)
            pe.wait_ge(s_efl, 1)
            for a in range(2):
                for t in range(4):
                    last = pe.transpose(p_tab[a][:, t * RC:(t + 1) * RC], edge_f[:, a, t, :], ident[0:RC, 0:RC])
            last.then_inc(s_tabT, 1)
            pe.wait_ge(s_viol, 1)
            pe.wait_ge(s_tab, 1)
            pe.matmul(ps[0:1, 6, 0:1], lim[:, 2:3], ones[:, :], start=True, stop=True).then_inc(s_vsum, 1)
            pe.wait_ge(s_vecs, 48)
            pe.transpose(ps[:, 7, 0:3 * KH], vec_rows[:, :], ident[0:3 * KH, 0:3 * KH]).then_inc(s_vecT, 1)
            for t in range(NT):
                if t % XT == 0:
                    pe.wait_ge(s_h32, t // XT + 1)
                if t >= 2:
                    pe.wait_ge(s_hTc, t - 1)
                for f in range(KD):
                    last = pe.transpose(p_tr[t % 2][:, f, :], h32[0:NP, t, f * P:(f + 1) * P], ident[0:NP, 0:NP])
                last.then_inc(s_hTp, 1)

            pe.wait_ge(s_flag, 1)
            irregular = pe.value_load(flag[0:1, 0:1], min_val=0, max_val=1)
            pe.wait_ge(s_w1, 16)

            def hidden(col, n, k, m):
                pe.wait_ge(s_h1, FREE + m - 2)
                for f in range(KD):
                    last = pe.matmul(p_hid[k % 2][:, 0:n], w1[:, f, k * P:(k + 1) * P],
                                     hT[:, f, bass.ds(BACK + col, n)], start=(f == 0), stop=(f == KD - 1))
                last.then_inc(s_hid, 1)

            def hidden_first(k):
                for f in range(KD):
                    last = pe.matmul(p_hid[k % 2][:, :], w1[:, f, k * P:(k + 1) * P],
                                     hT[:, f, BACK:BACK + NB], start=(f == 0), stop=(f == KD - 1))
                last.then_inc(s_hid, 1)

            with pe.If(irregular == 0):
                def group(q, g, r):
                    pe.wait_ge(s_gath[q], 16 * CG * (r + 1))
                    pe.wait_ge(s_hot, g + 1)
                    pe.wait_ge(s_add, g - 1)
                    group_products(q)

                def group_products(q):
                    for f in range(KD):
                        for c in range(CG):
                            for s in range(PARTS):
                                o = s * D + f * P
                                last = pe.matmul(p_win[q % 2][:, f, :], g_ring[:, q, c, o:o + P],
                                                 d_ring[:, q, c, :], start=(c + s == 0),
                                                 stop=(c == CG - 1 and s == PARTS - 1))
                    last.then_inc(s_win, 1)

                for q in range(Q):
                    pe.wait_ge(s_gath[q], 16 * CG)
                    pe.wait_ge(s_hot, q + 1)
                    if q >= 2:
                        pe.wait_ge(s_add, q - 1)
                    group_products(q)
                with pe.Fori(1, SUP // Q) as r:
                    for q in range(Q):
                        group(q, r * Q + q, r)
                with pe.Fori(1, NSUP) as J:
                    for j in range(SUP):
                        group(j % Q, J * SUP + j, J * (SUP // Q) + j // Q)
                        k = j - FIRST_HID
                        if 0 <= k < KH:
                            if k == 0:
                                pe.wait_ge(s_add, J * SUP + FIRST_HID)
                            hidden((J - 1) * NB, NB, k, (J - 1) * KH + k + 1)
                done = (NSUP - 1) * KH
                g0 = NSUP * SUP
                for j in range(G - g0):
                    group(j % Q, g0 + j, g0 // Q)
                    if j == 0:
                        pe.wait_ge(s_add, g0 - 2)
                    for k in range(j * KH // 2, (j + 1) * KH // 2):
                        hidden(*TAIL_A, k, done + k + 1)
                pe.wait_ge(s_add, G)
                for k in range(KH):
                    hidden(*TAIL_B, k, done + KH + k + 1)
            with pe.Else():
                pe.sem_inc(s_gused, 1)
                for f in range(KD):
                    if f:
                        pe.wait_ge(s_gadd, f)
                    else:
                        pe.wait_ge(s_hTc, NT)
                        pe.wait_ge(s_vec, 1)
                    for b in range(GB):
                        pe.matmul(ps[:, b, :], zcols[:, 0:P], zcols[:, :], start=True, stop=False)
                    with pe.Fori(0, C) as c:
                        pe.wait_ge(s_ggath, 16 * (f * C + c + 1))
                        pe.wait_ge(s_ghot, f * C + c + 1)
                        for s in range(PARTS):
                            o = s * D + f * P
                            for b in range(GB):
                                n = min(NB, N - b * NB)
                                last = pe.matmul(ps[:, b, 0:n], g_ring[:, 0, 0, o:o + P],
                                                 onehot_all[:, b * NB:b * NB + n], start=False, stop=False)
                        last.then_inc(s_gused, 1)
                    for b in range(GB):
                        last = pe.matmul(ps[:, b, :], zcols[:, 0:P], zcols[:, :], start=False, stop=True)
                    last.then_inc(s_gopen, 1)
                pe.wait_ge(s_gadd, KD)
                for k in range(KH):
                    pe.wait_ge(s_h1, FREE + k - 1)
                    hidden_first(k)
                with pe.Fori(1, NSUP - 1) as J:
                    for k in range(KH):
                        hidden(J * NB, NB, k, J * KH + k + 1)
                done = (NSUP - 1) * KH
                for k in range(KH):
                    hidden(*TAIL_A, k, done + k + 1)
                for k in range(KH):
                    hidden(*TAIL_B, k, done + KH + k + 1)

            pe.wait_ge(s_w2, 16)

            def product(b, k0, first):
                for s in range(2):
                    for k in range(KH):
                        if s == 0:
                            pe.wait_ge(s_hn, k0 + k + 1)
                        last = pe.matmul(p_out[b][:, s, :], hn[:, b, k, s * P:(s + 1) * P], w2[:, k, :],
                                         start=(k == 0), stop=(k == KH - 1))
                last.then_inc(s_out, 1)

            for b in (0, 1):
                product(b, b * KH, True)
            with pe.Fori(1, NSUP) as i:
                for b in (0, 1):
                    pe.wait_ge(s_bias, 2 * i + b - 1)
                    product(b, (2 * i + b) * KH, False)
            pe.wait_ge(s_bias, 2 * NSUP - 1)
            for k in range(KH):
                pe.wait_ge(s_hn, 2 * NSUP * KH + k + 1)
                last = pe.matmul(p_out[0][0:REST, 0, :], hn[:, 0, k, 0:REST], w2[:, k, :],
                                 start=(k == 0), stop=(k == KH - 1))
            last.then_inc(s_out, 1)

        @block.scalar
        def _(act):
            rows3 = (3 * RC) * P
            whole = E // P - 3 * RC
            left = E - (E // P) * P
            for a, e in enumerate((src, dst)):
                act.dma_start(edge_i[:, a, 0:3, :],
                              e[0:rows3].rearrange("(t c e) -> c t e", t=3, e=P)).then_inc(s_edges, 16)
                act.dma_start(edge_i[0:whole, a, 3, :],
                              e[rows3:rows3 + whole * P].rearrange("(c e) -> c e", e=P)).then_inc(s_edges, 16)
            act.wait_ge(s_pads, 2)
            for a, e in enumerate((src, dst)):
                act.dma_start(edge_i[whole:whole + 1, a, 3, 0:left],
                              e[E - left:E].rearrange("(c e) -> c e", c=1)).then_inc(s_edges, 16)
            for v, e in enumerate((b1, gamma, beta)):
                act.dma_start(vec_rows[v * KH:(v + 1) * KH, :], e.rearrange("(k p) -> k p", p=P)).then_inc(s_vecs, 16)
            act.wait_ge(s_const, 5)
            act.dma_start(h_rows[N:N + 1, :], zrow[:, :]).then_inc(s_hrow, 16)
            act.dma_start(w1[:, :, :], W1.rearrange("(k p) h -> p k h", p=P)).then_inc(s_w1, 16)

            for g in range(XG):
                ts = slice(g * XT, (g + 1) * XT)
                act.wait_ge(s_var, g + 1)
                act.activation(std[:, ts], mv[:, ts, 1], ACT.Sqrt, bias=epst[0:NP, :]).then_inc(s_std, 1)
                act.wait_ge(s_norm, g + 1)
                for t in range(g * XT, (g + 1) * XT):
                    last = act.activation(h32[0:NP, t, :], x_sb[0:NP, t, :], ACT.Relu,
                                          bias=nbias[:, t:t + 1], scale=rstd[:, t:t + 1])
                last.then_inc(s_h32, 1)
                act.wait_ge(s_h32, g + 1)
                act.activation(hp[:, ts, 0, :], h32[0:NP, ts, :], ACT.Copy).then_inc(s_hi, 1)
                act.wait_ge(s_res, g + 1)
                act.activation(hp[:, ts, 1, :], res[:, :, :], ACT.Copy).then_inc(s_mid, 1)
            for t in range(NT):
                act.wait_ge(s_hTp, t + 1)
                act.activation(hT[:, :, BACK + t * NP:BACK + (t + 1) * NP], p_tr[t % 2][:, :, :],
                               ACT.Copy).then_inc(s_hTc, 1)

            act.wait_ge(s_flag, 1)
            irregular = act.value_load(flag[0:1, 0:1], min_val=0, max_val=1)
            act.wait_ge(s_vec, 1)
            act.wait_ge(s_pad, 5)
            act.sem_inc(s_h1, FREE)

            def store_hidden(col, n, k, m):
                act.wait_ge(s_hid, m)
                act.activation(h1[:, k, bass.ds(col, n)], p_hid[k % 2][:, 0:n], ACT.Identity,
                               bias=vec[:, k:k + 1]).then_inc(s_h1, 1)

            with act.If(irregular == 0):
                def indices(q, g):
                    act.activation(idx_ring[:, q, :], src_tab[:, bass.ds(g * CG, CG)], ACT.Copy).then_inc(s_idx, 1)

                for q in range(Q):
                    indices(q, q)

                def refill(q, r):
                    act.wait_ge(s_gath[q], 16 * CG * (r + 1))
                    indices(q, (r + 1) * Q + q)

                with act.Fori(0, SUP // Q) as r:
                    for q in range(Q):
                        refill(q, r)
                with act.Fori(1, NSUP) as J:
                    for j in range(SUP):
                        refill(j % Q, J * (SUP // Q) + j // Q)
                        k = j - FIRST_HID
                        if 0 <= k < KH:
                            store_hidden((J - 1) * NB, NB, k, (J - 1) * KH + k + 1)
            with act.Else():
                with act.Fori(0, NSUP - 1) as J:
                    for k in range(KH):
                        store_hidden(J * NB, NB, k, J * KH + k + 1)
            done = (NSUP - 1) * KH
            for b, blk in enumerate((TAIL_A, TAIL_B)):
                for k in range(KH):
                    store_hidden(*blk, k, done + b * KH + k + 1)

            act.wait_ge(s_bvar, 1)
            act.activation(bstd[:, :], bmv[:, :, 1], ACT.Sqrt, bias=epst[:, :]).then_inc(s_bsd, 1)
            act.wait_ge(s_bn, 1)

            def normalise(b, col, n):
                for k in range(KH):
                    act.activation(hn[:, b, k, 0:n], h1[:, k, bass.ds(col, n)], ACT.Relu,
                                   bias=bshift[:, k:k + 1], scale=bscale[:, k:k + 1]).then_inc(s_hn, 1)

            for b in (0, 1):
                normalise(b, b * HALF, HALF)
            with act.Fori(1, NSUP) as i:
                for b in (0, 1):
                    act.wait_ge(s_out, 2 * i + b - 1)
                    normalise(b, i * NB + b * HALF, HALF)
            act.wait_ge(s_out, 2 * NSUP - 1)
            normalise(0, NSUP * NB, REST)

        @block.vector
        def _(dve):
            step = [0]

            def chain(ins):
                step[0] += 1
                ins.then_inc(s_dve, 1)
                dve.wait_ge(s_dve, step[0])

            def layer_stats(g):
                dve.wait_ge(s_x[g], 32)
                for t in range(g * XT, (g + 1) * XT):
                    last = dve.bn_stats(stats[:, t, :], x_sb[0:NP, t, :])
                chain(last)
                for t in range(g * XT, (g + 1) * XT):
                    last = dve.bn_aggr(mv[:, t, :], stats[:, t, :])
                last.then_inc(s_var, 1)

            def layer_parts(g):
                ts = slice(g * XT, (g + 1) * XT)
                dve.wait_ge(s_std, g + 1)
                chain(dve.reciprocal(rstd[:, ts], std[:, ts]))
                dve.scalar_tensor_tensor(nbias[:, ts], mv[:, ts, 0], -1.0, rstd[:, ts],
                                         ALU.mult, ALU.mult).then_inc(s_norm, 1)

            def layer_residue(g):
                ts = slice(g * XT, (g + 1) * XT)
                dve.wait_ge(s_hi, g + 1)
                if g:
                    dve.wait_ge(s_lo, g)
                dve.tensor_tensor(res[:, :, :], h32[0:NP, ts, :], hp[:, ts, 0, :],
                                  ALU.subtract).then_inc(s_res, 1)
                dve.wait_ge(s_mid, g + 1)
                dve.tensor_tensor(hp[:, ts, 2, :], res[:, :, :], hp[:, ts, 1, :],
                                  ALU.subtract).then_inc(s_lo, 1)

            layer_stats(0)
            layer_parts(0)
            dve.wait_ge(s_edges, 96)
            dve.tensor_copy(edge_f[:, :, :, :], edge_i[:, :, :, :]).then_inc(s_efl, 1)
            dve.wait_ge(s_const, 5)
            dve.tensor_copy(iota_f[:, :], iota_i[:, :])
            chain(dve.tensor_copy(win_f[:, :, :], win_i[:, :, :]))
            layer_stats(1)
            dve.wait_ge(s_tabT, 1)
            dve.tensor_copy(src_tab[:, 0:C], p_tab[0][:, :])
            dve.tensor_copy(dst_tab[:, :], p_tab[1][:, :])
            chain(dve.tensor_tensor(dst_rel[:, 0:C], p_tab[1][:, :], win_f[:, :, :].rearrange("p g c -> p (g c)"),
                                    ALU.subtract))
            dve.tensor_reduce(lim[:, 0:1], dst_rel[:, 0:C], AX.X, ALU.max)
            chain(dve.tensor_reduce(lim[:, 1:2], dst_rel[:, 0:C], AX.X, ALU.min))
            chain(dve.tensor_scalar(lim[:, 3:4], lim[:, 0:1], float(W - 1), None, ALU.is_gt))
            chain(dve.scalar_tensor_tensor(lim[:, 2:3], lim[:, 1:2], 0.0, lim[:, 3:4], ALU.is_lt, ALU.add))
            dve.engine_nop().then_inc(s_tab, 1)
            dve.engine_nop().then_inc(s_viol, 1)
            dve.wait_ge(s_vsum, 1)
            dve.tensor_scalar(flag[:, :], ps[0:1, 6, 0:1], 1.0, None, ALU.min).then_inc(s_flag, 1)
            dve.wait_ge(s_vecT, 1)
            dve.tensor_copy(vec[:, :], ps[:, 7, 0:3 * KH]).then_inc(s_vec, 1)
            layer_residue(0)
            for g in range(1, XG):
                layer_parts(g)
                if g + 1 < XG:
                    layer_stats(g + 1)
                layer_residue(g)

            dve.wait_ge(s_flag, 1)
            irregular = dve.value_load(flag[0:1, 0:1], min_val=0, max_val=1)
            dve.wait_ge(s_pad, 5)

            def hidden_stats(col, n, k, j, m):
                dve.wait_ge(s_h1, FREE + m)
                return dve.bn_stats(bst[:, k, j, :], h1[:, k, bass.ds(col, n)])

            bst_v = bst[:, :, :, :].rearrange("p k j s -> p k (j s)")

            def hidden_stats_at(J, k, m):
                dve.wait_ge(s_h1, FREE + m)
                dve.bn_stats(bst_v[:, k, bass.ds(J * 6, 6)], h1[:, k, bass.ds(J * NB, NB)])

            with dve.If(irregular == 0):
                iota_b = iota_f[:, :].unsqueeze(1).to_broadcast([P, CG, W])

                def onehots(q, g):
                    rel = dst_rel[:, bass.ds(g * CG, CG)].unsqueeze(2).to_broadcast([P, CG, W])
                    dve.tensor_tensor(d_ring[:, q, :, :], iota_b, rel, ALU.is_equal).then_inc(s_hot, 1)

                def add_window(q, g):
                    dve.wait_ge(s_win, g + 1)
                    w = hT[:, :, bass.ds(g * STEP, W)]
                    dve.tensor_tensor(w, w, p_win[q % 2][:, :, :], ALU.add).then_inc(s_add, 1)

                def group(q, g):
                    dve.wait_ge(s_add, g)
                    add_window(q, g)

                for q in range(Q):
                    onehots(q, q)
                dve.wait_ge(s_hTc, NT)
                add_window(0, 0)
                onehots(0, Q)
                for q in range(1, Q):
                    group(q, q)
                    onehots(q, Q + q)
                with dve.Fori(1, SUP // Q) as r:
                    for q in range(Q):
                        group(q, r * Q + q)
                        onehots(q, r * Q + Q + q)
                with dve.Fori(1, NSUP) as J:
                    for j in range(SUP):
                        group(j % Q, J * SUP + j)
                        onehots(j % Q, J * SUP + j + Q)
                        k = j - FIRST_HID - 1
                        if 0 <= k < KH:
                            hidden_stats_at(J - 1, k, (J - 1) * KH + k + 1)
                for g in range(NSUP * SUP, G):
                    group(g % Q, g)
            with dve.Else():
                dve.wait_ge(s_giota, 1)
                dve.tensor_copy(node_iota, node_iota.bitcast(I32)).then_inc(s_giota, 1)
                dve.wait_ge(s_giota, 2)
                for f in range(KD):
                    with dve.Fori(0, C) as c:
                        dve.wait_ge(s_gused, f * C + c + 1)
                        dve.tensor_copy(idx_ring[:, 0, 0:1], src_tab[:, bass.ds(c, 1)]).then_inc(s_gidx, 1)
                        dve.tensor_tensor(onehot_all, node_iota,
                                          dst_tab[:, bass.ds(c, 1)].to_broadcast([P, N]),
                                          ALU.is_equal).then_inc(s_ghot, 1)
                    dve.wait_ge(s_gopen, f + 1)
                    w = hT[:, f, BACK:BACK + N]
                    dve.wait_ge(s_hTc, NT)
                    for b in range(GB):
                        n = min(NB, N - b * NB)
                        wb = hT[:, f, BACK + b * NB:BACK + b * NB + n]
                        last = dve.tensor_tensor(wb, wb, ps[:, b, 0:n], ALU.add)
                    last.then_inc(s_gadd, 1)
                with dve.Fori(0, NSUP - 1) as J:
                    for k in range(KH):
                        hidden_stats_at(J, k, J * KH + k + 1)
            done = (NSUP - 1) * KH
            for b, blk in enumerate((TAIL_A, TAIL_B)):
                for k in range(KH):
                    last = hidden_stats(*blk, k, NSUP - 1 + b, done + b * KH + k + 1)
            chain(last)

            for k in range(KH):
                last = dve.bn_aggr(bmv[:, k, :], bst[:, k, :, :])
            last.then_inc(s_bvar, 1)
            dve.wait_ge(s_bsd, 1)
            chain(dve.reciprocal(brstd[:, :], bstd[:, :]))
            chain(dve.tensor_tensor(bscale[:, :], brstd[:, :], vec[:, KH:2 * KH], ALU.mult))
            chain(dve.tensor_tensor(bms[:, :], bmv[:, :, 0], bscale[:, :], ALU.mult))
            dve.tensor_tensor(bshift[:, :], vec[:, 2 * KH:3 * KH], bms[:, :], ALU.subtract).then_inc(s_bn, 1)

            dve.wait_ge(s_b2, 16)
            b2v = b2b[:, :].unsqueeze(1).to_broadcast([P, 2, D])

            def finish(b, m, r, first):
                dve.wait_ge(s_out, m)
                if not first:
                    dve.wait_ge(s_st[b], 16 * r)
                dve.tensor_tensor(o2[:, b, :, :], p_out[b][:, :, :], b2v, ALU.add).then_inc(s_bias, 1)
                dve.wait_ge(s_bias, m)
                dve.wait_ge(s_x2[b], 16 * (r + 1))
                dve.scalar_tensor_tensor(o2[:, b, :, :], o2[:, b, :, :], 0.0, x2[:, b, :, :],
                                         ALU.max, ALU.add).then_inc(s_o2, 1)

            for b in (0, 1):
                finish(b, b + 1, 0, True)
            with dve.Fori(1, NSUP) as i:
                for b in (0, 1):
                    finish(b, 2 * i + b + 1, i, False)
            m = 2 * NSUP + 1
            dve.wait_ge(s_out, m)
            dve.wait_ge(s_st[0], 16 * NSUP)
            dve.tensor_tensor(o2[0:REST, 0, 0, :], p_out[0][0:REST, 0, :], b2b[0:REST, :], ALU.add).then_inc(s_bias, 1)
            dve.wait_ge(s_bias, m)
            dve.wait_ge(s_x2[0], 16 * (NSUP + 1))
            dve.scalar_tensor_tensor(o2[0:REST, 0, 0, :], o2[0:REST, 0, 0, :], 0.0, x2[0:REST, 0, 0, :],
                                     ALU.max, ALU.add).then_inc(s_o2, 1)


_INS = ["x", "src", "dst", "L0_gnn_W1", "L0_gnn_b1", "L0_gnn_gamma", "L0_gnn_beta", "L0_gnn_W2", "L0_gnn_b2"]


def kernel(**inputs):
    import numpy as _np
    import concourse.bacc as _bacc
    from concourse import mybir as _mybir
    from concourse.bass_utils import run_bass_kernel_spmd as _run

    nc = _bacc.Bacc("TRN2", target_bir_lowering=False, num_devices=1)
    arrays, args = {}, []
    for name in _INS:
        a = _np.ascontiguousarray(inputs[name])
        arrays[f"in_{name}"] = a
        args.append(nc.dram_tensor(f"in_{name}", a.shape, _mybir.dt.from_np(a.dtype), kind="ExternalInput").ap())
    args.append(nc.dram_tensor("out_0", (N, D), F32, kind="ExternalOutput").ap())
    build(nc, *args)
    r = _run(nc, [arrays], core_ids=[0])
    return r.results[0]["out_0"]
```

```python
from contextlib import ExitStack

import concourse.bass as bass
from concourse import mybir

F32 = mybir.dt.float32
F16 = mybir.dt.float16
BF16 = mybir.dt.bfloat16
I32 = mybir.dt.int32
ALU = mybir.AluOpType
ACT = mybir.ActivationFunctionType
AX = mybir.AxisListType

N, D, H, E = 3125, 256, 1024, 50000
EPS = 1e-5
P = 128
KD, KH = D // P, H // P

NP = 125
NT = N // NP
XT = 5
XG = NT // XT
SPLIT = [3] * (XG - 1) + [4]
LO = 112

CG = 4
G = -(-E // (P * CG))
C = G * CG
RC = C // 4
STEP = 32
W = 96
BACK = 32
PARTS = 3
ROW = PARTS * D
HTW = STEP * (G - 1) + W

NB = 512
PAIR = 2 * NB
NPAIR = N // PAIR
REST = N - NPAIR * PAIR
NSTAT = 2 * NPAIR + 1
GP = PAIR // STEP
D0, D1 = 18, 30
DC = (D1 - D0) * CG
DB = DC // CG
LB = 6
SLOTS = GP - (D1 - D0)
TAIL = G - NPAIR * GP
NG = NPAIR * SLOTS + TAIL
AHEAD = 2
XS = 10
DW = 14
KEYS = NT * DW
DEG = 14
MAGIC = 1.5 * 2.0 ** 23

PADS = 3 + NPAIR + 1
FREE = 2
Q = 4
TR = 6
HALF = NB // 2
NSUP = N // NB
GB = -(-N // NB)


def gathered_group(s):
    over, s = divmod(s, SLOTS)
    return GP * over + (s if s < D0 else s + D1 - D0)


def count_batches(s, lead):
    if not lead:
        return range(DB * s // XS, DB * (s + 1) // XS)
    return range(AHEAD) if s < 0 else range(AHEAD + (DB - AHEAD) * s // XS, AHEAD + (DB - AHEAD) * (s + 1) // XS)


def slot_work(s, lead):
    chunks = [("count", k, c) for k in count_batches(s, lead) for c in range(CG)]
    n = 2 * KH * KD
    products = [] if lead else [("hidden", j // KD, j % KD) for j in range(n * s // XS, n * (s + 1) // XS)]
    placed = ([((j + 0.5) / len(chunks), w) for j, w in enumerate(chunks)] +
              [((j + 0.5) / len(products), w) for j, w in enumerate(products)])
    return [w for _, w in sorted(placed)]


def build(nc, x, src, dst, W1, b1, gamma, beta, W2, b2, out):
    h_rows = nc.dram_tensor("h_rows", [N + 1, ROW], BF16).ap()
    ctx = ExitStack()
    with ctx:
        def sb(name, shape, dt):
            return ctx.enter_context(nc.sbuf_tensor(name, shape, dt))

        def sem(name):
            return ctx.enter_context(nc.semaphore(name))

        h1T = sb("h1T", [P, KH * HTW], F32)
        h1 = h1T[:, :].rearrange("p (k n) -> p k n", k=KH)
        hT = h1[:, KH - KD:KH, :]
        x_sb = h1T[:, 0:NT * D].rearrange("p (t d) -> p t d", t=NT)
        h32 = h1T[:, NT * D:2 * NT * D].rearrange("p (t d) -> p t d", t=NT)
        node_iota = h1T[:, 0:N]
        onehot_all = h1T[:, N + 1:N + 1 + (N + 1) // 2].bitcast(BF16)[:, 0:N]
        at = 2 * NT * D
        edge_i = h1T[0:RC, at:at + 8 * P].bitcast(I32).rearrange("p (a t e) -> p a t e", a=2, t=4)
        at += 8 * P
        quot = h1T[:, at - 8 * P:at - 8 * P + C]
        pos_f = h1T[:, at - 8 * P + C:at - 8 * P + 2 * C]
        edge_f = h1T[0:RC, at:at + 8 * P].rearrange("p (a t e) -> p a t e", a=2, t=4)
        dst_tab = h1T[:, at:at + C]
        grow = (h1T[:, at + C:at + C + NPAIR * (DC - DEG)]
                .rearrange("p (i c) -> p i c", i=NPAIR))
        at += 8 * P
        res = h1T[0:NP, at:at + 2 * XT * D].rearrange("p (b t d) -> p b t d", b=2, t=XT)
        at += 2 * XT * D
        win_f = h1T[:, at:at + C]
        at += C
        blk_f = h1T[:, at:at + C]
        at += C
        late = BACK + (NPAIR - 1) * PAIR
        stats = h1T[0:NP, at:at + 6 * NT].rearrange("p (t s) -> p t s", t=NT)
        at += 6 * NT
        mv = h1T[0:NP, at:at + 2 * NT].rearrange("p (t s) -> p t s", t=NT)
        at += 2 * NT
        std, rstd, nbias = (h1T[0:NP, at + v * NT:at + (v + 1) * NT] for v in range(3))
        at += 3 * NT
        assert at <= (KH - KD) * HTW
        key_ring = (h1[:, 0, late:late + CG * KEYS // 2].bitcast(F16)
                    .rearrange("p (c k) -> p c k", c=CG))
        sq = h1[:, KH - KD - 2, late:late + CG * P].rearrange("p (c r) -> p c r", c=CG)
        src_ring = (h1[:, KH - KD - 2, late + CG * P:late + 2 * CG * P].bitcast(BF16)
                    .rearrange("p (b c r) -> p b c r", b=2, c=CG))
        d_ring = []
        for row, nth in ((KH - KD - 1, 0), (KH - KD - 1, 1), (KH - KD - 1, 2), (1, 0)):
            o = late + NB + nth * (CG * W // 2)
            assert o + CG * W // 2 <= HTW
            d_ring.append(h1[:, row, o:o + CG * W // 2].bitcast(BF16).rearrange("p (c w) -> p c w", c=CG))
        hp = sb("hp", [NP, NT, PARTS, D], BF16)
        w1 = sb("w1", [P, KD, H], F32)
        counts = sb("counts", [P, NT, NB], F16)
        zeros = counts[:, :, :].rearrange("p t n -> p (t n)").bitcast(BF16)
        zcols = zeros[:, 0:NB]
        flat = counts[:, :, :].rearrange("p t n -> p (t n)").bitcast(F32)
        w2 = flat[:, 0:KH * D].rearrange("p (k d) -> p k d", k=KH)
        b2b = flat[:, (KH + 4) * D:(KH + 5) * D]
        x2 = flat[:, KH * D:KH * D + 4 * D].rearrange("p (b s d) -> p b s d", b=2, s=2)
        vec_rows = sb("vec_rows", [3 * KH, P], F32)
        vec = sb("vec", [P, 3 * KH], F32)
        ident = sb("ident", [P, P], F32)
        ones = sb("ones", [P, 1], F32)
        epst = sb("epst", [P, 1], F32)
        src_tab = sb("src_tab", [P, C], I32)
        dst_rel = sb("dst_rel", [P, C], F32)
        neg_rem = sb("neg_rem", [P, C], F32)
        key = sb("key", [P, C], F32)
        pos = sb("pos", [1, C], I32)
        iota_k = sb("iota_k", [P, KEYS], F16)
        iota_f = sb("iota_f", [P, P], F32)
        lim = sb("lim", [P, 16], F32)
        flag = sb("flag", [1, 1], I32)
        idx_ring = sb("idx_ring", [P, Q, CG], I32)
        g_ring = sb("g_ring", [P, Q, CG, ROW], BF16)
        row0 = g_ring[:, 0, 0, 0:2 * P].bitcast(F32)
        bst = sb("bst", [P, KH, NSTAT, 6], F32)
        bmv = sb("bmv", [P, KH, 2], F32)
        bstd = sb("bstd", [P, KH], F32)
        brstd = sb("brstd", [P, KH], F32)
        bscale = sb("bscale", [P, KH], F32)
        bms = sb("bms", [P, KH], F32)
        bshift = sb("bshift", [P, KH], F32)
        over = g_ring[:, :, :, :].rearrange("p q c r -> p (q c r)").bitcast(F32)
        hn = over[:, 0:2 * KH * HALF].rearrange("p (b k n) -> p b k n", b=2, k=KH)
        o2 = over[:, 2 * KH * HALF:2 * KH * HALF + 4 * D].rearrange("p (b s d) -> p b s d", b=2, s=2)

        def high(ap):
            return ap.bitcast(BF16).rearrange("p t (d two) -> p t d two", two=2)[:, :, :, 1]

        ps = ctx.enter_context(nc.psum_tensor("ps", [P, 8, NB], F32))
        p_win = [ps[:, b, 0:KD * W].rearrange("p (f w) -> p f w", f=KD) for b in (0, 1)]
        p_hid = [ps[:, b, :] for b in (2, 3)]
        p_cnt = [ps[:, b, 0:KEYS].rearrange("p (t w) -> p t w", t=NT) for b in range(4, 8)]
        p_agg = [ps[:, b, :] for b in (6, 7)]
        p_tr = [ps[:, b, 0:KD * NP].rearrange("p (f n) -> p f n", f=KD) for b in range(TR)]
        p_tab = [ps[:, b, 0:C] for b in (6, 7)]
        p_out = [ps[:, b, :].rearrange("p (s d) -> p s d", s=2) for b in (4, 5)]

        s_x = [sem(f"x_loaded{g}") for g in range(XG)]
        s_edges = sem("edges_loaded")
        s_vecs = sem("vecs_loaded")
        s_w1 = sem("w1_loaded")
        s_w2 = sem("w2_loaded")
        s_b2 = sem("b2_loaded")
        s_hrow = sem("h_rows_stored")
        s_const = sem("consts_made")
        s_pads = sem("pads_made")
        s_ident = sem("ident_made")
        s_efl = sem("edges_as_float")
        s_tabT = sem("tables_transposed")
        s_viol = sem("violations_known")
        s_vsum = sem("violations_summed")
        s_flag = sem("flag_ready")
        s_row0 = sem("row0_made")
        s_dtab = sem("dst_table_ready")
        s_first = sem("first_dst_everywhere")
        s_vecT = sem("vecs_transposed")
        s_vec = sem("vecs_ready")
        s_var = sem("variances_ready")
        s_std = sem("stds_ready")
        s_norm = sem("norms_ready")
        s_h32 = sem("h_made")
        s_hi = sem("hi_made")
        s_res = sem("residue_made")
        s_mid = sem("mid_made")
        s_lo = sem("lo_made")
        s_resp = sem("residue_made_by_pool")
        s_midp = sem("mid_made_by_pool")
        s_lop = sem("lo_made_by_pool")
        s_hTp = sem("h_transposed")
        s_hTc = sem("hT_copied")
        s_pad = sem("hT_pads_zero")
        s_dve = sem("dve_step")
        s_idx = sem("indices_ready")
        s_turn = sem("pool_turn")
        s_gath = [sem(f"gathered{q}") for q in range(Q)]
        s_hot = sem("onehots_ready")
        s_win = sem("window_summed")
        s_add = sem("window_added")
        s_key = sem("keys_ready")
        s_src = sem("src_onehots_ready")
        s_sq = sem("squares_ready")
        s_cnt = sem("chunk_counted")
        s_cadd = sem("counts_added")
        s_agg = sem("counts_times_h")
        s_zero = sem("counts_zeroed")
        s_aadd = sem("block_added")
        s_used = sem("counts_used_up")
        s_hid = sem("hidden_computed")
        s_h1 = sem("hidden_stored")
        s_bst = sem("hidden_stats")
        s_gidx = sem("general_index_ready")
        s_ggath = sem("general_gathered")
        s_ghot = sem("general_onehot_ready")
        s_giota = sem("general_iota_ready")
        s_gused = sem("general_chunk_used")
        s_gopen = sem("general_sums_closed")
        s_gadd = sem("general_added")
        s_bvar = sem("bn_var_ready")
        s_bsd = sem("bn_std_ready")
        s_bn = sem("bn_ready")
        s_hn = sem("normalised")
        s_out = sem("outputs_computed")
        s_x2 = [sem(f"residual_loaded{b}") for b in (0, 1)]
        s_bias = sem("bias_added")
        s_o2 = sem("outputs_ready")
        s_st = [sem(f"stored{b}") for b in (0, 1)]

        block = ctx.enter_context(nc.Block())

        def residue(eng, g, ts, rs, res_made, lo_made, mid_made=None):
            eng.wait_ge(s_h32, g + 1)
            r = res[:, g % 2, rs, :]
            if g >= 2:
                if mid_made is None:
                    eng.wait_ge(s_mid, g - 1)
                eng.wait_ge(s_midp, g - 1)
                eng.wait_ge(s_lop, g - 1)
            eng.tensor_tensor(r, h32[0:NP, ts, :], high(h32[0:NP, ts, :]), ALU.subtract).then_inc(res_made, 1)
            eng.wait_ge(res_made, g + 1)
            if mid_made is not None:
                eng.tensor_copy(hp[:, ts, 1, :], high(r)).then_inc(mid_made, 1)
            eng.tensor_tensor(hp[:, ts, 2, :], r, high(r), ALU.subtract).then_inc(lo_made, 1)

        def x_view(dram, g):
            rows = dram[g * XT * NP:(g + 1) * XT * NP, :]
            return rows.rearrange("(t p) d -> p t d", p=NP)

        def tail_rows(dram):
            return dram[NSUP * NB:N, :]

        @block.sync
        def _(sp):
            def load_x(g):
                v = x_view(x, g)
                for a, b in ((0, LO), (LO, NP)):
                    sp.dma_start(x_sb[a:b, g * XT:(g + 1) * XT, :], v[a:b]).then_inc(s_x[g], 16)

            load_x(0)
            load_x(1)
            rows3 = (3 * RC) * P
            whole = E // P - 3 * RC
            left = E - (E // P) * P
            for a, e in enumerate((src, dst)):
                sp.dma_start(edge_i[:, a, 0:3, :],
                             e[0:rows3].rearrange("(t c e) -> c t e", t=3, e=P)).then_inc(s_edges, 16)
                sp.dma_start(edge_i[0:whole, a, 3, :],
                             e[rows3:rows3 + whole * P].rearrange("(c e) -> c e", e=P)).then_inc(s_edges, 16)
            sp.wait_ge(s_pads, 2)
            for a, e in enumerate((src, dst)):
                sp.dma_start(edge_i[whole:whole + 1, a, 3, 0:left],
                             e[E - left:E].rearrange("(c e) -> c e", c=1)).then_inc(s_edges, 16)
            for g in range(2, XG):
                load_x(g)
            for v, e in enumerate((b1, gamma, beta)):
                sp.dma_start(vec_rows[v * KH:(v + 1) * KH, :], e.rearrange("(k p) -> k p", p=P)).then_inc(s_vecs, 16)
            sp.wait_ge(s_zero, 1)
            sp.dma_start(h_rows[N:N + 1, :], zeros[0:1, 0:ROW]).then_inc(s_hrow, 16)
            sp.dma_start(w1[:, :, :], W1.rearrange("(k p) h -> p k h", p=P)).then_inc(s_w1, 16)
            for g in range(XG):
                sp.wait_ge(s_lop, g + 1)
                sp.wait_ge(s_lo, g + 1)
                sp.wait_ge(s_mid, g + 1)
                sp.wait_ge(s_midp, g + 1)
                sp.wait_ge(s_hi, g + 1)
                v = x_view(h_rows, g)
                for a, b in ((0, LO), (LO, NP)):
                    sp.dma_start(v[a:b], hp[a:b, g * XT:(g + 1) * XT, :, :]
                                 .rearrange("p t s d -> p t (s d)")).then_inc(s_hrow, 16)

            def load(row0, b):
                sp.dma_start(x2[:, b, :, :],
                             x[bass.ds(row0, HALF), :].rearrange("(s p) d -> p s d", p=P)).then_inc(s_x2[b], 16)

            def store(row0, b):
                sp.dma_start(out[bass.ds(row0, HALF), :].rearrange("(s p) d -> p s d", p=P),
                             o2[:, b, :, :]).then_inc(s_st[b], 16)

            sp.wait_ge(s_used, 1)
            sp.dma_start(w2[:, :, :], W2.rearrange("(k p) d -> p k d", p=P)).then_inc(s_w2, 16)
            sp.dma_start(b2b[:, :], b2.rearrange("(a d) -> a d", a=1).to_broadcast([P, D])).then_inc(s_b2, 16)
            for b in (0, 1):
                load(b * HALF, b)
            with sp.Fori(0, NSUP - 1) as i:
                for b in (0, 1):
                    sp.wait_ge(s_o2, 2 * i + b + 1)
                    store(i * NB + b * HALF, b)
                    load((i + 1) * NB + b * HALF, b)
            for b in (0, 1):
                sp.wait_ge(s_o2, 2 * (NSUP - 1) + b + 1)
                store((NSUP - 1) * NB + b * HALF, b)
                if b == 0:
                    sp.dma_start(x2[0:REST, 0, 0, :], tail_rows(x)).then_inc(s_x2[0], 16)
            sp.wait_ge(s_o2, 2 * NSUP + 1)
            sp.dma_start(tail_rows(out), o2[0:REST, 0, 0, :]).then_inc(s_st[0], 16)
            sp.wait_ge(s_st[0], 16 * (NSUP + 1))
            sp.wait_ge(s_st[1], 16 * NSUP)

        @block.gpsimd
        def _(pool):
            pool.memset(edge_i[RC - 2:RC, 0, 3, :], N).then_inc(s_pads, 1)
            pool.wait_ge(s_pads, 1)
            pool.memset(edge_i[RC - 2:RC, 1, 3, :], N - 1).then_inc(s_pads, 1)
            pool.wait_ge(s_pads, 2)
            pool.memset(ident[:, :], 0.0).then_inc(s_ident, 1)
            pool.memset(ones[:, :], 1.0).then_inc(s_const, 1)
            pool.memset(epst[:, :], EPS).then_inc(s_const, 1)
            loose = dict(channel_multiplier=0, allow_small_or_imprecise_dtypes=True)
            pool.iota(iota_f[:, :], pattern=[[1, P]], base=0, **loose).then_inc(s_const, 1)
            pool.iota(win_f.rearrange("p (g c) -> p g c", c=CG), pattern=[[STEP, G], [0, CG]],
                      base=-BACK, **loose).then_inc(s_const, 1)
            pool.wait_ge(s_ident, 1)
            pool.affine_select(out=ident[:, :], in_=ident[:, :], compare_op=ALU.not_equal, fill=1.0, base=0,
                               pattern=[[-1, P]], channel_multiplier=1).then_inc(s_ident, 1)
            pool.memset(row0[:, :], 0.0).then_inc(s_row0, 1)
            pool.wait_ge(s_row0, 1)
            pool.memset(row0[0:1, :], 1.0).then_inc(s_row0, 1)
            for i in range(NPAIR):
                pool.iota(blk_f[:, i * GP * CG:(i + 1) * GP * CG], pattern=[[0, GP * CG]],
                          base=i * PAIR + NB, **loose).then_inc(s_pad, 1)
            pool.memset(blk_f[:, NPAIR * GP * CG:C], 0.0).then_inc(s_pad, 1)
            pool.memset(counts[:, :, :].bitcast(I32), 0).then_inc(s_zero, 1)
            pool.wait_ge(s_edges, 96)
            pool.tensor_copy(edge_f[:, :, :, :], edge_i[:, :, :, :]).then_inc(s_efl, 1)
            pool.memset(hT[:, :, 0:BACK], 0.0).then_inc(s_pad, 1)
            pool.memset(hT[:, :, BACK + N:HTW], 0.0).then_inc(s_pad, 1)
            pool.iota(iota_k[:, :], pattern=[[1, KEYS]], base=0, **loose).then_inc(s_pad, 1)

            for g in range(XG):
                residue(pool, g, slice(g * XT + SPLIT[g], (g + 1) * XT), slice(SPLIT[g], XT), s_resp, s_lop, s_midp)

            pool.wait_ge(s_flag, 1)
            irregular = pool.value_load(flag[0:1, 0:1], min_val=0, max_val=1)
            pool.wait_ge(s_hrow, 16 * (2 * XG + 1))

            def gather(to, index, done):
                pool.indirect_dma_start(to, None, h_rows,
                                        bass.IndirectOffsetOnAxis(ap=index, axis=0)).then_inc(done, 16)

            with pool.If(irregular == 0):
                def group(q, g, first):
                    pool.wait_ge(s_idx, g + 1)
                    if not first:
                        pool.wait_ge(s_win, g - Q + 1)
                    pool.sem_inc(s_turn, 1)
                    for c in range(CG):
                        gather(g_ring[:, q, c, :], idx_ring[:, q, c:c + 1], s_gath[q])

                for q in range(Q):
                    group(q, q, True)
                with pool.Fori(1, NG // Q) as r:
                    for q in range(Q):
                        group(q, r * Q + q, False)
                for g in range(NG // Q * Q, NG):
                    group(g % Q, g, False)
            with pool.Else():
                pool.iota(node_iota.bitcast(I32), pattern=[[1, N]], base=0,
                          channel_multiplier=0).then_inc(s_giota, 1)
                with pool.Fori(0, KD * C) as c:
                    pool.wait_ge(s_gidx, c + 1)
                    pool.sem_inc(s_turn, 1)
                    gather(g_ring[:, 0, 0, :], idx_ring[:, 0, 0:1], s_ggath)

        @block.tensor
        def _(pe):
            pe.wait_ge(s_ident, 2)
            pe.wait_ge(s_efl, 1)
            for a in range(2):
                for t in range(4):
                    last = pe.transpose(p_tab[a][:, t * RC:(t + 1) * RC], edge_f[:, a, t, :], ident[0:RC, 0:RC])
            last.then_inc(s_tabT, 1)
            pe.wait_ge(s_row0, 2)
            pe.wait_ge(s_dtab, 1)
            pe.matmul(p_tab[0][:, :], row0[:, :], dst_tab[:, :], start=True, stop=True).then_inc(s_first, 1)
            pe.wait_ge(s_vecs, 48)
            pe.transpose(ps[:, 7, 0:3 * KH], vec_rows[:, :], ident[0:3 * KH, 0:3 * KH]).then_inc(s_vecT, 1)
            for t in range(NT):
                if t % XT == 0:
                    pe.wait_ge(s_h32, t // XT + 1)
                if t >= TR:
                    pe.wait_ge(s_hTc, t - TR + 1)
                for f in range(KD):
                    last = pe.transpose(p_tr[t % TR][:, f, :], h32[0:NP, t, f * P:(f + 1) * P], ident[0:NP, 0:NP])
                last.then_inc(s_hTp, 1)
                if t == NT - TR - 1:
                    pe.wait_ge(s_viol, 1)
                    pe.matmul(ps[0:1, 6, 0:1], lim[:, 0:1], ones[:, :], start=True, stop=True).then_inc(s_vsum, 1)

            pe.wait_ge(s_flag, 1)
            irregular = pe.value_load(flag[0:1, 0:1], min_val=0, max_val=1)
            pe.wait_ge(s_w1, 16)

            def hidden(col, n, k, m, fs=range(KD)):
                for f in fs:
                    if f == 0:
                        pe.wait_ge(s_h1, FREE + m - 2)
                    last = pe.matmul(p_hid[k % 2][:, 0:n], w1[:, f, k * P:(k + 1) * P],
                                     hT[:, f, bass.ds(BACK + col, n)], start=(f == 0), stop=(f == KD - 1))
                    if f == KD - 1:
                        last.then_inc(s_hid, 1)

            with pe.If(irregular == 0):
                def group(i, s, lead=False):
                    n, q = i * SLOTS + s, s % Q
                    r = i * (SLOTS // Q) + s // Q
                    pe.wait_ge(s_gath[q], (r + 1) * (16 * CG))
                    pe.wait_ge(s_hot, n + 1)
                    if not lead or s >= 2:
                        pe.wait_ge(s_add, n - 1)
                    for f in range(KD):
                        for c in range(CG):
                            for p in range(PARTS):
                                o = p * D + f * P
                                last = pe.matmul(p_win[q % 2][:, f, :], g_ring[:, q, c, o:o + P],
                                                 d_ring[q][:, c, :], start=(c + p == 0),
                                                 stop=(c == CG - 1 and p == PARTS - 1))
                    last.then_inc(s_win, 1)

                def count(i, k, c, lead):
                    m = i * DC + k * CG + c
                    if c == 0:
                        pe.wait_ge(s_src, i * DB + k + 1)
                        if not lead and k == 0:
                            pe.wait_ge(s_aadd, i)
                    pe.wait_ge(s_key, m + 1)
                    if not lead or k:
                        pe.wait_ge(s_cadd, m - CG + 1)
                    pe.matmul(ps[:, 4 + c, 0:KEYS], src_ring[:, k % 2, c, :], key_ring[:, c, :],
                              start=True, stop=True).then_inc(s_cnt, 1)

                def times_h(i, s):
                    e = s - XS
                    t0, t1 = (NT * x // (SLOTS - XS) for x in (e, e + 1))
                    if e == 0:
                        pe.wait_ge(s_cadd, (i + 1) * DC)
                    for t in range(t0, t1):
                        for p in range(PARTS):
                            for f in range(KD):
                                last = pe.matmul(p_agg[f], hp[:, t, p, f * P:(f + 1) * P], counts[0:NP, t, :],
                                                 start=(t + p == 0), stop=(t == NT - 1 and p == PARTS - 1))
                    last.then_inc(s_agg, 1)

                def hidden_of_pair(i, h, f):
                    if h + f == 0:
                        pe.wait_ge(s_add, i * SLOTS + D0)
                    if h == KH and f == 0:
                        pe.wait_ge(s_add, (i + 1) * SLOTS + TAIL)
                        pe.wait_ge(s_aadd, i + 1)
                    hidden(i * PAIR + h // KH * NB, NB, h % KH, i * (2 * KH) + h + 1, (f,))

                def counting_slot(i, s, lead):
                    if s >= 0:
                        group(i, s, lead)
                    for what, a, b in slot_work(s, lead):
                        if what == "count":
                            count(i, a, b, lead)
                        else:
                            hidden_of_pair(i - 1, a, b)

                pe.wait_ge(s_hTc, NT)
                for s in range(-1, XS):
                    counting_slot(0, s, True)
                with pe.Fori(0, NPAIR - 1) as i:
                    for s in range(XS, SLOTS):
                        group(i, s)
                        times_h(i, s)
                    for s in range(XS):
                        counting_slot(i + 1, s, False)
                i = NPAIR - 1
                for s in range(XS, SLOTS):
                    group(i, s)
                    times_h(i, s)
                for h in range(2 * KH):
                    if h in (KH // 2, KH):
                        group(i, SLOTS + (h > KH // 2))
                    for f in range(KD):
                        hidden_of_pair(i, h, f)
            with pe.Else():
                pe.sem_inc(s_gused, 1)
                pe.wait_ge(s_zero, 1)
                for f in range(KD):
                    if f:
                        pe.wait_ge(s_gadd, f)
                    else:
                        pe.wait_ge(s_hTc, NT)
                        pe.wait_ge(s_vec, 1)
                    for b in range(GB):
                        pe.matmul(ps[:, b, :], zcols[:, 0:P], zcols[:, :], start=True, stop=False)
                    with pe.Fori(0, C) as c:
                        pe.wait_ge(s_ggath, 16 * (f * C + c + 1))
                        pe.wait_ge(s_ghot, f * C + c + 1)
                        for s in range(PARTS):
                            o = s * D + f * P
                            for b in range(GB):
                                n = min(NB, N - b * NB)
                                last = pe.matmul(ps[:, b, 0:n], g_ring[:, 0, 0, o:o + P],
                                                 onehot_all[:, b * NB:b * NB + n], start=False, stop=False)
                        last.then_inc(s_gused, 1)
                    for b in range(GB):
                        last = pe.matmul(ps[:, b, :], zcols[:, 0:P], zcols[:, :], start=False, stop=True)
                    last.then_inc(s_gopen, 1)
                pe.wait_ge(s_gadd, KD)
                with pe.Fori(0, NSUP) as J:
                    for k in range(KH):
                        hidden(J * NB, NB, k, J * KH + k + 1)
            for k in range(KH):
                hidden(NSUP * NB, REST, k, NSUP * KH + k + 1)

            pe.wait_ge(s_w2, 16)

            def product(b, k0, first):
                for s in range(2):
                    for k in range(KH):
                        if s == 0:
                            pe.wait_ge(s_hn, k0 + k + 1)
                        last = pe.matmul(p_out[b][:, s, :], hn[:, b, k, s * P:(s + 1) * P], w2[:, k, :],
                                         start=(k == 0), stop=(k == KH - 1))
                last.then_inc(s_out, 1)

            for b in (0, 1):
                product(b, b * KH, True)
            with pe.Fori(1, NSUP) as i:
                for b in (0, 1):
                    pe.wait_ge(s_bias, 2 * i + b - 1)
                    product(b, (2 * i + b) * KH, False)
            pe.wait_ge(s_bias, 2 * NSUP - 1)
            for k in range(KH):
                pe.wait_ge(s_hn, 2 * NSUP * KH + k + 1)
                last = pe.matmul(p_out[0][0:REST, 0, :], hn[:, 0, k, 0:REST], w2[:, k, :],
                                 start=(k == 0), stop=(k == KH - 1))
            last.then_inc(s_out, 1)

        @block.scalar
        def _(act):
            act.wait_ge(s_const, 4)
            act.activation(bstd[:, 0:1], epst[:, :], ACT.Sqrt)

            def middle(g):
                act.wait_ge(s_res, g + 1)
                act.activation(hp[:, g * XT:g * XT + SPLIT[g], 1, :], high(res[:, g % 2, 0:SPLIT[g], :]),
                               ACT.Copy).then_inc(s_mid, 1)

            def deviations(g):
                ts = slice(g * XT, (g + 1) * XT)
                act.wait_ge(s_var, g + 1)
                act.activation(std[:, ts], mv[:, ts, 1], ACT.Sqrt, bias=epst[0:NP, :]).then_inc(s_std, 1)

            deviations(0)
            for g in range(XG):
                ts = slice(g * XT, (g + 1) * XT)
                act.wait_ge(s_norm, g + 1)
                for t in range(g * XT, (g + 1) * XT):
                    last = act.activation(h32[0:NP, t, :], x_sb[0:NP, t, :], ACT.Relu,
                                          bias=nbias[:, t:t + 1], scale=rstd[:, t:t + 1])
                last.then_inc(s_h32, 1)
                if g + 1 < XG:
                    deviations(g + 1)
                act.wait_ge(s_h32, g + 1)
                act.activation(hp[:, ts, 0, :], high(h32[0:NP, ts, :]), ACT.Copy).then_inc(s_hi, 1)
                if g:
                    middle(g - 1)
            middle(XG - 1)

            def indices(q, g):
                act.activation(idx_ring[:, q, :], src_tab[:, bass.ds(g * CG, CG)], ACT.Copy).then_inc(s_idx, 1)

            act.wait_ge(s_dtab, 1)
            for q in range(Q):
                indices(q, q)
            for t in range(NT):
                act.wait_ge(s_hTp, t + 1)
                act.activation(hT[:, :, BACK + t * NP:BACK + (t + 1) * NP], p_tr[t % TR][:, :, :],
                               ACT.Copy).then_inc(s_hTc, 1)

            act.wait_ge(s_flag, 1)
            irregular = act.value_load(flag[0:1, 0:1], min_val=0, max_val=1)
            act.wait_ge(s_vec, 1)
            act.wait_ge(s_pad, PADS)
            act.sem_inc(s_h1, FREE)

            def store_hidden(col, n, k, m):
                act.wait_ge(s_hid, m + 1 if k == KH - KD else m)
                act.activation(h1[:, k, bass.ds(BACK + col, n)], p_hid[k % 2][:, 0:n], ACT.Identity,
                               bias=vec[:, k:k + 1]).then_inc(s_h1, 1)

            with act.If(irregular == 0):
                def refill(i, s):
                    q = s % Q
                    act.wait_ge(s_gath[q], (i * (SLOTS // Q) + s // Q + 1) * (16 * CG))
                    indices(q, i * GP + gathered_group(s + Q))

                def src_onehots(i, k, lead):
                    m = i * DB + k
                    if not lead or k:
                        act.wait_ge(s_src, m)
                    for c in range(CG):
                        at = (i * (GP * CG) + D0 * CG) + k * CG + c
                        last = act.activation(sq[:, c, :], iota_f[:, :], ACT.Square,
                                              bias=neg_rem[:, bass.ds(at, 1)])
                    last.then_inc(s_sq, 1)
                    act.wait_ge(s_sq, m + 1)
                    if not lead or k >= 2:
                        act.wait_ge(s_cnt, (m - 1) * CG)
                    act.activation(src_ring[:, k % 2, :, :], sq[:, :, :], ACT.Relu, bias=1.0,
                                   scale=-1.0).then_inc(s_src, 1)

                def store_tiles(i, h):
                    for g in ([h - 1, h] if h % KH == KH - 1 else [h] if h % KH < KH - 2 else []):
                        store_hidden(i * PAIR + g // KH * NB, NB, g % KH, i * (2 * KH) + g + 1)

                def counting_slot(i, s, lead):
                    if s >= 0:
                        refill(i, s)
                    for what, a, b in slot_work(s, lead):
                        if what == "count" and b == 0 and a + 1 < DB:
                            src_onehots(i, a + 1, lead)
                        if what == "hidden" and b == KD - 1:
                            store_tiles(i - 1, a)

                act.wait_ge(s_viol, 1)
                act.wait_ge(s_lo, XG)
                act.wait_ge(s_lop, XG)
                src_onehots(0, 0, True)
                for s in range(-1, XS):
                    counting_slot(0, s, True)
                with act.Fori(0, NPAIR - 1) as i:
                    for s in range(XS, SLOTS):
                        refill(i, s)
                    src_onehots(i + 1, 0, False)
                    for s in range(XS):
                        counting_slot(i + 1, s, False)
                i = NPAIR - 1
                for s in range(XS, SLOTS + TAIL - Q):
                    refill(i, s)
                for h in range(2 * KH):
                    store_tiles(i, h)
            with act.Else():
                with act.Fori(0, NSUP) as J:
                    for k in range(KH):
                        store_hidden(J * NB, NB, k, J * KH + k + 1)
            for k in range(KH):
                store_hidden(NSUP * NB, REST, k, NSUP * KH + k + 1)

            act.wait_ge(s_bvar, 1)
            act.activation(bstd[:, :], bmv[:, :, 1], ACT.Sqrt, bias=epst[:, :]).then_inc(s_bsd, 1)
            act.wait_ge(s_bn, 1)

            def normalise(b, col, n):
                for k in range(KH):
                    act.activation(hn[:, b, k, 0:n], h1[:, k, bass.ds(BACK + col, n)], ACT.Relu,
                                   bias=bshift[:, k:k + 1], scale=bscale[:, k:k + 1]).then_inc(s_hn, 1)

            for b in (0, 1):
                normalise(b, b * HALF, HALF)
            with act.Fori(1, NSUP) as i:
                for b in (0, 1):
                    act.wait_ge(s_out, 2 * i + b - 1)
                    normalise(b, i * NB + b * HALF, HALF)
            act.wait_ge(s_out, 2 * NSUP - 1)
            normalise(0, NSUP * NB, REST)

        @block.vector
        def _(dve):
            step = [0]

            def chain(ins):
                step[0] += 1
                ins.then_inc(s_dve, 1)
                dve.wait_ge(s_dve, step[0])

            def layer_stats(g):
                dve.wait_ge(s_x[g], 32)
                for t in range(g * XT, (g + 1) * XT):
                    last = dve.bn_stats(stats[:, t, :], x_sb[0:NP, t, :])
                chain(last)
                for t in range(g * XT, (g + 1) * XT):
                    last = dve.bn_aggr(mv[:, t, :], stats[:, t, :])
                last.then_inc(s_var, 1)

            def layer_parts(g):
                ts = slice(g * XT, (g + 1) * XT)
                dve.wait_ge(s_std, g + 1)
                chain(dve.reciprocal(rstd[:, ts], std[:, ts]))
                dve.scalar_tensor_tensor(nbias[:, ts], mv[:, ts, 0], -1.0, rstd[:, ts],
                                         ALU.mult, ALU.mult).then_inc(s_norm, 1)

            def layer_residue(g):
                residue(dve, g, slice(g * XT, g * XT + SPLIT[g]), slice(0, SPLIT[g]), s_res, s_lo)

            def edge_tables():
                dve.wait_ge(s_tabT, 1)
                dve.tensor_copy(src_tab[:, :], p_tab[0][:, :])
                dve.tensor_scalar(quot[:, :], p_tab[0][:, :], 1.0 / NP, -(NP // 2) / NP, ALU.mult, ALU.add)
                dve.tensor_copy(neg_rem[:, :], p_tab[0][:, :])
                dve.tensor_copy(dst_tab[:, :], p_tab[1][:, :]).then_inc(s_dtab, 1)

            counted = slice(D0 * CG, D1 * CG)

            def counted_part(t):
                return t[:, 0:NPAIR * GP * CG].rearrange("p (i c) -> p i c", i=NPAIR)[:, :, counted]

            span, where = counted_part(key), counted_part(pos_f)
            values = [(dst_rel[:, :], 0, W - 1), (span, 0, DW - 1), (where, 0, NB - DW),
                      (grow[:, :, :], 1, None)]

            def tables_relative():
                dve.wait_ge(s_const, 4)
                dve.wait_ge(s_pad, NPAIR + 1)
                dve.wait_ge(s_first, 1)
                first = p_tab[0]
                chain(dve.tensor_scalar(quot[:, :], quot[:, :], MAGIC, MAGIC, ALU.add, ALU.subtract))
                dve.tensor_tensor(dst_rel[:, :], dst_tab[:, :], win_f, ALU.subtract)
                dve.tensor_tensor(key[:, :], dst_tab[:, :], first[:, :], ALU.subtract)
                dve.tensor_tensor(pos_f[:, :], first[:, :], blk_f, ALU.subtract)
                chain(dve.scalar_tensor_tensor(neg_rem[:, :], quot[:, :], float(NP), neg_rem[:, :],
                                               ALU.mult, ALU.subtract))
                dve.tensor_copy(pos[:, :], pos_f[0:1, :])
                steps = where.shape[2] - DEG
                chain(dve.tensor_tensor(grow[:, :, :], where[:, :, DEG:], where[:, :, 0:steps], ALU.subtract))

            def tables_extremes():
                for v, (t, least, most) in enumerate(values):
                    axis = AX.X if len(t.shape) == 2 else AX.XY
                    dve.tensor_reduce(lim[:, 4 + 2 * v:5 + 2 * v], t, axis, ALU.min)
                    last = dve.tensor_reduce(lim[:, 5 + 2 * v:6 + 2 * v], t, axis, ALU.max)
                chain(last)

            def tables_checked():
                for v, (t, least, most) in enumerate(values):
                    if v == 0:
                        chain(dve.tensor_scalar(lim[:, v:v + 1], lim[:, 4:5], float(least), None, ALU.is_lt))
                    else:
                        chain(dve.scalar_tensor_tensor(lim[:, 0:1], lim[:, 4 + 2 * v:5 + 2 * v], float(least),
                                                       lim[:, 0:1], ALU.is_lt, ALU.add))
                    if most is not None:
                        chain(dve.scalar_tensor_tensor(lim[:, 0:1], lim[:, 5 + 2 * v:6 + 2 * v], float(most),
                                                       lim[:, 0:1], ALU.is_gt, ALU.add))
                dve.scalar_tensor_tensor(key[:, :], quot[:, :], float(DW), key[:, :], ALU.mult,
                                         ALU.add).then_inc(s_viol, 1)

            layer_stats(0)
            layer_parts(0)
            layer_stats(1)
            layer_parts(1)
            for g in range(2, XG):
                layer_stats(g)
                layer_parts(g)
                layer_residue(g - 2)
            edge_tables()
            layer_residue(XG - 2)
            tables_relative()
            dve.wait_ge(s_vecT, 1)
            dve.tensor_copy(vec[:, :], ps[:, 7, 0:3 * KH]).then_inc(s_vec, 1)
            layer_residue(XG - 1)
            tables_extremes()
            tables_checked()
            dve.wait_ge(s_vsum, 1)
            dve.tensor_scalar(flag[:, :], ps[0:1, 6, 0:1], 1.0, None, ALU.min).then_inc(s_flag, 1)

            dve.wait_ge(s_flag, 1)
            irregular = dve.value_load(flag[0:1, 0:1], min_val=0, max_val=1)
            dve.wait_ge(s_pad, PADS)

            def hidden_stats(col, n, k, j, m):
                dve.wait_ge(s_h1, FREE + m)
                return dve.bn_stats(bst[:, k, j, :], h1[:, k, bass.ds(BACK + col, n)])

            bst_v = bst[:, :, :, :].rearrange("p k j s -> p k (j s)")

            def hidden_stats_at(J, k, m):
                dve.wait_ge(s_h1, FREE + m)
                dve.bn_stats(bst_v[:, k, bass.ds(J * 6, 6)], h1[:, k, bass.ds(BACK + J * NB, NB)])

            with dve.If(irregular == 0):
                iota_b = iota_f[:, 0:W].unsqueeze(1).to_broadcast([P, CG, W])

                def onehots(q, g):
                    rel = dst_rel[:, bass.ds(g * CG, CG)].unsqueeze(2).to_broadcast([P, CG, W])
                    dve.tensor_tensor(d_ring[q], iota_b, rel, ALU.is_equal).then_inc(s_hot, 1)

                def window(i, s, last, lead=False):
                    n, q = i * SLOTS + s, s % Q
                    if not lead or s:
                        dve.wait_ge(s_add, n)
                    if s % SLOTS < TAIL and not lead:
                        dve.wait_ge(s_aadd, i + s // SLOTS)
                    dve.wait_ge(s_win, n + 1)
                    w = hT[:, :, bass.ds((i * GP + gathered_group(s)) * STEP, W)]
                    dve.tensor_tensor(w, w, p_win[q % 2][:, :, :], ALU.add).then_inc(s_add, 1)
                    if not last:
                        onehots(q, i * GP + gathered_group(s + Q))

                def count_step(i, k, c, lead):
                    m = i * DC + k * CG + c
                    if k:
                        add_counts(m - CG, c, added_at(i, k - 1, c), lead and k == 1 and c == 0)
                    if k < DB:
                        at = (i * (GP * CG) + D0 * CG) + k * CG + c
                        dve.tensor_scalar(key_ring[:, c, :], iota_k[:, :], key[:, bass.ds(at, 1)], None,
                                          ALU.is_equal).then_inc(s_key, 1)

                positions = []

                def added_at(i, k, c):
                    if k % LB == 0 and c == 0:
                        at = (i * (GP * CG) + D0 * CG) + k * CG
                        _, positions[:] = nc.values_load_multi_w_load_instructions(
                            pos[0:1, bass.ds(at, LB * CG)], engines=[dve.engine], min_val=0, max_val=NB - DW,
                            skip_runtime_bounds_check_because="the regular path has checked them")
                    return positions[k % LB * CG + c]

                def counting_slot(i, s, lead):
                    work = [(k, c) for k in count_batches(s, lead) for c in range(CG)]
                    for j, (k, c) in enumerate(work):
                        if j == len(work) // 2 and s >= 0:
                            window(i, s, False, lead)
                        count_step(i, k, c, lead)

                def last_batch(i, lead):
                    for c in range(CG):
                        count_step(i, DB, c, lead)

                def add_counts(m, c, where, first):
                    if not first:
                        dve.wait_ge(s_cadd, m)
                    dve.wait_ge(s_cnt, m + 1)
                    a = counts[:, :, bass.ds(where, DW)]
                    dve.tensor_tensor(a, a, p_cnt[c], ALU.add).then_inc(s_cadd, 1)

                def add_block(i):
                    dve.wait_ge(s_agg, (i + 1) * (SLOTS - XS))
                    dve.wait_ge(s_add, (i + 1) * SLOTS)
                    b = hT[:, :, bass.ds(BACK + i * PAIR + NB, NB)]
                    dve.tensor_tensor(b, b, ps[:, 6:8, :], ALU.add).then_inc(s_aadd, 1)

                def zero_counts(i, s):
                    e = s - XS
                    t0, t1 = (NT * x // (SLOTS - XS) for x in (e, e + 1))
                    dve.wait_ge(s_agg, i * (SLOTS - XS) + e + 1)
                    dve.memset(counts[:, t0:t1, :].bitcast(I32), 0).then_inc(s_zero, 1)

                def stats_of(i, h):
                    hidden_stats_at(i * 2 + h // KH, h % KH, i * (2 * KH) + h + 1)

                for q in range(Q):
                    onehots(q, gathered_group(q))
                dve.wait_ge(s_zero, 1)
                dve.wait_ge(s_hTc, NT)
                for s in range(-1, XS):
                    counting_slot(0, s, True)
                last_batch(0, True)
                with dve.Fori(0, NPAIR - 1) as i:
                    for s in range(XS, SLOTS):
                        window(i, s, False)
                        zero_counts(i, s)
                    add_block(i)
                    dve.wait_ge(s_zero, (i + 1) * (SLOTS - XS) + 1)
                    for s in range(XS):
                        counting_slot(i + 1, s, False)
                    last_batch(i + 1, False)
                i = NPAIR - 1
                before = [(j, h) for j in range(i) for h in range(2 * KH)]
                for s in range(XS, SLOTS):
                    window(i, s, s + Q >= SLOTS + TAIL)
                    e, n = s - XS, SLOTS - XS
                    for j, h in before[len(before) * e // n:len(before) * (e + 1) // n]:
                        stats_of(j, h)
                dve.wait_ge(s_agg, NPAIR * (SLOTS - XS))
                dve.sem_inc(s_used, 1)
                add_block(i)
                for h in range(2 * KH):
                    if h in (KH // 2, KH):
                        window(i, SLOTS + (h > KH // 2), True)
                    stats_of(i, h)
            with dve.Else():
                dve.wait_ge(s_giota, 1)
                dve.wait_ge(s_idx, Q)
                dve.tensor_copy(node_iota, node_iota.bitcast(I32)).then_inc(s_giota, 1)
                dve.wait_ge(s_giota, 2)
                for f in range(KD):
                    with dve.Fori(0, C) as c:
                        dve.wait_ge(s_gused, f * C + c + 1)
                        dve.tensor_copy(idx_ring[:, 0, 0:1], src_tab[:, bass.ds(c, 1)]).then_inc(s_gidx, 1)
                        dve.tensor_tensor(onehot_all, node_iota,
                                          dst_tab[:, bass.ds(c, 1)].to_broadcast([P, N]),
                                          ALU.is_equal).then_inc(s_ghot, 1)
                    dve.wait_ge(s_gopen, f + 1)
                    if f == KD - 1:
                        dve.sem_inc(s_used, 1)
                    w = hT[:, f, BACK:BACK + N]
                    dve.wait_ge(s_hTc, NT)
                    for b in range(GB):
                        n = min(NB, N - b * NB)
                        wb = hT[:, f, BACK + b * NB:BACK + b * NB + n]
                        last = dve.tensor_tensor(wb, wb, ps[:, b, 0:n], ALU.add)
                    last.then_inc(s_gadd, 1)
                with dve.Fori(0, NSUP) as J:
                    for k in range(KH):
                        hidden_stats_at(J, k, J * KH + k + 1)
            for k in range(KH):
                last = hidden_stats(NSUP * NB, REST, k, NSUP, NSUP * KH + k + 1)
            chain(last)

            for k in range(KH):
                last = dve.bn_aggr(bmv[:, k, :], bst[:, k, :, :])
            last.then_inc(s_bvar, 1)
            dve.wait_ge(s_bsd, 1)
            chain(dve.reciprocal(brstd[:, :], bstd[:, :]))
            chain(dve.tensor_tensor(bscale[:, :], brstd[:, :], vec[:, KH:2 * KH], ALU.mult))
            chain(dve.tensor_tensor(bms[:, :], bmv[:, :, 0], bscale[:, :], ALU.mult))
            dve.tensor_tensor(bshift[:, :], vec[:, 2 * KH:3 * KH], bms[:, :], ALU.subtract).then_inc(s_bn, 1)

            dve.wait_ge(s_b2, 16)
            b2v = b2b[:, :].unsqueeze(1).to_broadcast([P, 2, D])

            def finish(b, m, r, first):
                dve.wait_ge(s_out, m)
                if not first:
                    dve.wait_ge(s_st[b], 16 * r)
                dve.tensor_tensor(o2[:, b, :, :], p_out[b][:, :, :], b2v, ALU.add).then_inc(s_bias, 1)
                dve.wait_ge(s_bias, m)
                dve.wait_ge(s_x2[b], 16 * (r + 1))
                dve.scalar_tensor_tensor(o2[:, b, :, :], o2[:, b, :, :], 0.0, x2[:, b, :, :],
                                         ALU.max, ALU.add).then_inc(s_o2, 1)

            for b in (0, 1):
                finish(b, b + 1, 0, True)
            with dve.Fori(1, NSUP) as i:
                for b in (0, 1):
                    finish(b, 2 * i + b + 1, i, False)
            m = 2 * NSUP + 1
            dve.wait_ge(s_out, m)
            dve.wait_ge(s_st[0], 16 * NSUP)
            dve.tensor_tensor(o2[0:REST, 0, 0, :], p_out[0][0:REST, 0, :], b2b[0:REST, :], ALU.add).then_inc(s_bias, 1)
            dve.wait_ge(s_bias, m)
            dve.wait_ge(s_x2[0], 16 * (NSUP + 1))
            dve.scalar_tensor_tensor(o2[0:REST, 0, 0, :], o2[0:REST, 0, 0, :], 0.0, x2[0:REST, 0, 0, :],
                                     ALU.max, ALU.add).then_inc(s_o2, 1)


_INS = ["x", "src", "dst", "L0_gnn_W1", "L0_gnn_b1", "L0_gnn_gamma", "L0_gnn_beta", "L0_gnn_W2", "L0_gnn_b2"]


def kernel(**inputs):
    import numpy as _np
    import concourse.bacc as _bacc
    from concourse import mybir as _mybir
    from concourse.bass_utils import run_bass_kernel_spmd as _run

    nc = _bacc.Bacc("TRN2", target_bir_lowering=False, num_devices=1)
    arrays, args = {}, []
    for name in _INS:
        a = _np.ascontiguousarray(inputs[name])
        arrays[f"in_{name}"] = a
        args.append(nc.dram_tensor(f"in_{name}", a.shape, _mybir.dt.from_np(a.dtype), kind="ExternalInput").ap())
    args.append(nc.dram_tensor("out_0", (N, D), F32, kind="ExternalOutput").ap())
    build(nc, *args)
    r = _run(nc, [arrays], core_ids=[0])
    return r.results[0]["out_0"]
```

```python
from contextlib import ExitStack

import concourse.bass as bass
from concourse import mybir

F32 = mybir.dt.float32
F16 = mybir.dt.float16
BF16 = mybir.dt.bfloat16
I32 = mybir.dt.int32
ALU = mybir.AluOpType
ACT = mybir.ActivationFunctionType
AX = mybir.AxisListType

N, D, H, E = 3125, 256, 1024, 50000
EPS = 1e-5
P = 128
KD, KH = D // P, H // P

NP = 125
NT = N // NP
XT = 5
XG = NT // XT
SPLIT = [3] * XG
LO = 112

CG = 4
G = -(-E // (P * CG))
C = G * CG
RC = C // 4
STEP = 32
W = 48
SLACK = 32
PARTS = 3
ROW = PARTS * D
HTW = N + W + 3

NB = 512
PAIR = 2 * NB
NPAIR = N // PAIR
REST = N - NPAIR * PAIR
NSTAT = 2 * NPAIR + 1
GP = PAIR // STEP
D0, D1 = 18, 30
DC = (D1 - D0) * CG
DB = DC // CG
LB = 6
SLOTS = GP - (D1 - D0)
TAIL = G - NPAIR * GP
NG = NPAIR * SLOTS + TAIL
TAIL_AT = (2, 4)
CX = C + 2 * CG
AHEAD = 2
XS = 10
DW = 14
KEYS = NT * DW
DEG = 14
MAGIC = 1.5 * 2.0 ** 23

LEAST = (0, 0, 0, 1, 0)
MOST = (W - 1, DW - 1, NB - DW)

PADS = 12 + NPAIR + 1
FREE = 2
Q = 4
TR = 6
HALF = NB // 2
NSUP = N // NB
GB = -(-N // NB)


def gathered_group(s):
    over, s = divmod(s, SLOTS)
    return GP * over + (s if s < D0 else s + D1 - D0)


def count_batches(s, lead):
    ahead = AHEAD if lead else 0
    first, last = (ahead + (DB - ahead) * x // XS for x in (s, s + 1))
    return range(ahead) if s < 0 else range(first, last)


def slot_work(s, lead):
    chunks = [("count", k, c) for k in count_batches(s, lead) for c in range(CG)]
    n = 0 if lead else 2 * KH * KD
    products = [("hidden", j // KD, j % KD) for j in range(n * s // XS, n * (s + 1) // XS)]
    placed = ([((j + 0.7) / len(chunks), w) for j, w in enumerate(chunks)] +
              [((j + 0.3) / len(products), w) for j, w in enumerate(products)])
    return [w for _, w in sorted(placed)]


def build(nc, x, src, dst, W1, b1, gamma, beta, W2, b2, out):
    h_rows = nc.dram_tensor("h_rows", [N + 1, ROW], BF16).ap()
    ctx = ExitStack()
    with ctx:
        def sb(name, shape, dt):
            return ctx.enter_context(nc.sbuf_tensor(name, shape, dt))

        def sem(name):
            return ctx.enter_context(nc.semaphore(name))

        h1T = sb("h1T", [P, KH * HTW], F32)
        h1 = h1T[:, :].rearrange("p (k n) -> p k n", k=KH)
        hT = h1[:, KH - KD:KH, :]
        x_sb = h1T[:, 0:NT * D].rearrange("p (t d) -> p t d", t=NT)
        h32 = h1T[:, NT * D:2 * NT * D].rearrange("p (t d) -> p t d", t=NT)
        node_iota = h1T[:, 0:N]
        onehot_all = h1T[:, N + 1:N + 1 + (N + 1) // 2].bitcast(BF16)[:, 0:N]
        at = 2 * NT * D
        edge_i = h1T[0:RC, at:at + 8 * P].bitcast(I32).rearrange("p (a t e) -> p a t e", a=2, t=4)
        at += 8 * P
        quot = h1T[:, at - 8 * P:at - 8 * P + C]
        pos_f = h1T[:, at - 8 * P + C:at - 8 * P + 2 * C]
        edge_f = h1T[0:RC, at:at + 8 * P].rearrange("p (a t e) -> p a t e", a=2, t=4)
        dst_tab = h1T[:, at:at + C]
        grow = (h1T[:, at + C:at + C + NPAIR * (DC - DEG)]
                .rearrange("p (i c) -> p i c", i=NPAIR))
        at += 8 * P
        res = h1T[0:NP, at:at + 2 * XT * D].rearrange("p (b t d) -> p b t d", b=2, t=XT)
        at += 2 * XT * D
        win_f = h1T[:, at:at + G]
        at += G
        blk_f = h1T[:, at:at + C]
        at += C
        late = (NPAIR - 1) * PAIR
        stats = h1T[0:NP, at:at + 6 * NT].rearrange("p (t s) -> p t s", t=NT)
        at += 6 * NT
        mv = h1T[0:NP, at:at + 2 * NT].rearrange("p (t s) -> p t s", t=NT)
        at += 2 * NT
        std, rstd, nbias = (h1T[0:NP, at + v * NT:at + (v + 1) * NT] for v in range(3))
        at += 3 * NT
        assert at <= (KH - KD) * HTW
        key_ring = (h1[:, 0, late:late + CG * KEYS // 2].bitcast(F16)
                    .rearrange("p (c k) -> p c k", c=CG))
        sq = h1[:, KH - KD - 2, late:late + CG * P].rearrange("p (c r) -> p c r", c=CG)
        src_ring = (h1[:, KH - KD - 2, late + CG * P:late + 2 * CG * P].bitcast(BF16)
                    .rearrange("p (b c r) -> p b c r", b=2, c=CG))
        d_ring = []
        for q in range(Q):
            o = late + NB + q * (CG * W // 2)
            assert o + CG * W // 2 <= HTW
            d_ring.append(h1[:, KH - KD - 1, o:o + CG * W // 2].bitcast(BF16)
                          .rearrange("p (c w) -> p c w", c=CG))
        hp = sb("hp", [NP, NT, PARTS, D], BF16)
        w1 = sb("w1", [P, KD, H], F32)
        counts = sb("counts", [P, NT, NB], F16)
        zeros = counts[:, :, :].rearrange("p t n -> p (t n)").bitcast(BF16)
        zcols = zeros[:, 0:NB]
        flat = counts[:, :, :].rearrange("p t n -> p (t n)").bitcast(F32)
        w2 = flat[:, 0:KH * D].rearrange("p (k d) -> p k d", k=KH)
        b2b = flat[:, (KH + 4) * D:(KH + 5) * D]
        x2 = flat[:, KH * D:KH * D + 4 * D].rearrange("p (b s d) -> p b s d", b=2, s=2)
        vec_rows = sb("vec_rows", [3 * KH, P], F32)
        vec = sb("vec", [P, 3 * KH], F32)
        ident = sb("ident", [P, P], F32)
        ones = sb("ones", [P, 1], F32)
        epst = sb("epst", [P, 1], F32)
        src_tab = sb("src_tab", [P, CX], I32)
        dst_rel = sb("dst_rel", [P, CX], F32)
        neg_rem = sb("neg_rem", [P, C], F32)
        key = sb("key", [P, C], F32)
        pos = sb("pos", [1, C], I32)
        start = sb("start", [1, G], I32)
        early = sb("early", [P, G], F32)
        iota_k = sb("iota_k", [P, KEYS], F16)
        iota_f = sb("iota_f", [P, P], F32)
        bounds = sb("bounds", [P, len(LEAST + MOST)], F32)
        found = sb("found", [P, len(LEAST + MOST)], F32)
        broken = sb("broken", [P, len(LEAST + MOST)], F32)
        flag = sb("flag", [1, 1], I32)
        idx_ring = sb("idx_ring", [P, Q, CG], I32)
        g_ring = sb("g_ring", [P, Q, CG, ROW], BF16)
        row0 = g_ring[:, 0, 0, 0:2 * P].bitcast(F32)
        bst = sb("bst", [P, KH, NSTAT, 6], F32)
        bmv = sb("bmv", [P, KH, 2], F32)
        bstd = sb("bstd", [P, KH], F32)
        brstd = sb("brstd", [P, KH], F32)
        bscale = sb("bscale", [P, KH], F32)
        bms = sb("bms", [P, KH], F32)
        bshift = sb("bshift", [P, KH], F32)
        over = g_ring[:, :, :, :].rearrange("p q c r -> p (q c r)").bitcast(F32)
        hn = over[:, 0:2 * KH * HALF].rearrange("p (b k n) -> p b k n", b=2, k=KH)
        o2 = over[:, 2 * KH * HALF:2 * KH * HALF + 4 * D].rearrange("p (b s d) -> p b s d", b=2, s=2)

        def high(ap):
            return ap.bitcast(BF16).rearrange("p t (d two) -> p t d two", two=2)[:, :, :, 1]

        ps = ctx.enter_context(nc.psum_tensor("ps", [P, 8, NB], F32))
        p_win = [ps[:, b, 0:KD * W].rearrange("p (f w) -> p f w", f=KD) for b in (0, 1)]
        p_hid = [ps[:, b, :] for b in (2, 3)]
        p_cnt = [ps[:, b, 0:KEYS].rearrange("p (t w) -> p t w", t=NT) for b in range(4, 8)]
        p_rest = [ps[:, 4 + k // 2, k % 2 * REST:(k % 2 + 1) * REST] for k in range(KH)]
        p_agg = [ps[:, b, :] for b in (6, 7)]
        p_tr = [ps[:, b, 0:KD * NP].rearrange("p (f n) -> p f n", f=KD) for b in range(TR)]
        p_tab = [ps[:, b, 0:C] for b in (6, 7)]
        p_out = [ps[:, b:b + 2, 0:D] for b in (4, 6)]

        s_x = [sem(f"x_loaded{g}") for g in range(XG)]
        s_edges = sem("edges_loaded")
        s_vecs = sem("vecs_loaded")
        s_w1 = sem("w1_loaded")
        s_w2 = sem("w2_loaded")
        s_b2 = sem("b2_loaded")
        s_hrow = sem("h_rows_stored")
        s_const = sem("consts_made")
        s_pads = sem("pads_made")
        s_ident = sem("ident_made")
        s_efl = sem("edges_as_float")
        s_tabT = sem("tables_transposed")
        s_viol = sem("violations_known")
        s_vsum = sem("violations_summed")
        s_flag = sem("flag_ready")
        s_row0 = sem("row0_made")
        s_dtab = sem("dst_table_ready")
        s_first = sem("first_dst_everywhere")
        s_vecT = sem("vecs_transposed")
        s_vec = sem("vecs_ready")
        s_var = sem("variances_ready")
        s_std = sem("stds_ready")
        s_norm = sem("norms_ready")
        s_h32 = sem("h_made")
        s_hi = sem("hi_made")
        s_res = sem("residue_made")
        s_mid = sem("mid_made")
        s_lo = sem("lo_made")
        s_resp = sem("residue_made_by_pool")
        s_midp = sem("mid_made_by_pool")
        s_lop = sem("lo_made_by_pool")
        s_hTp = sem("h_transposed")
        s_hTc = sem("hT_copied")
        s_pad = sem("hT_pads_zero")
        s_dve = sem("dve_step")
        s_idx = sem("indices_ready")
        s_turn = sem("pool_turn")
        s_gath = [sem(f"gathered{q}") for q in range(Q)]
        s_hot = sem("onehots_ready")
        s_win = sem("window_summed")
        s_add = sem("window_added")
        s_key = sem("keys_ready")
        s_src = sem("src_onehots_ready")
        s_sq = sem("squares_ready")
        s_cnt = sem("chunk_counted")
        s_cadd = sem("counts_added")
        s_agg = sem("counts_times_h")
        s_zero = sem("counts_zeroed")
        s_zrow = sem("zero_row_made")
        s_zst = sem("zero_row_stored")
        s_aadd = sem("block_added")
        s_used = sem("counts_used_up")
        s_hid = sem("hidden_computed")
        s_h1 = sem("hidden_stored")
        s_bst = sem("hidden_stats")
        s_rhid = sem("rest_computed")
        s_rh1 = sem("rest_stored")
        s_gidx = sem("general_index_ready")
        s_ggath = sem("general_gathered")
        s_ghot = sem("general_onehot_ready")
        s_giota = sem("general_iota_ready")
        s_gused = sem("general_chunk_used")
        s_gopen = sem("general_sums_closed")
        s_gadd = sem("general_added")
        s_bvar = sem("bn_var_ready")
        s_bsd = sem("bn_std_ready")
        s_bn = sem("bn_ready")
        s_hn = sem("normalised")
        s_out = sem("outputs_computed")
        s_x2 = [sem(f"residual_loaded{b}") for b in (0, 1)]
        s_bias = sem("bias_added")
        s_o2 = sem("outputs_ready")
        s_st = [sem(f"stored{b}") for b in (0, 1)]

        block = ctx.enter_context(nc.Block())

        def residue(eng, g, ts, rs, res_made, lo_made, mid_made=None):
            eng.wait_ge(s_h32, g + 1)
            r = res[:, g % 2, rs, :]
            if g >= 2:
                if mid_made is None:
                    eng.wait_ge(s_mid, g - 1)
                eng.wait_ge(s_midp, g - 1)
                eng.wait_ge(s_lop, g - 1)
            eng.tensor_tensor(r, h32[0:NP, ts, :], high(h32[0:NP, ts, :]), ALU.subtract).then_inc(res_made, 1)
            eng.wait_ge(res_made, g + 1)
            if mid_made is not None:
                eng.tensor_copy(hp[:, ts, 1, :], high(r)).then_inc(mid_made, 1)
            eng.tensor_tensor(hp[:, ts, 2, :], r, high(r), ALU.subtract).then_inc(lo_made, 1)

        def x_view(dram, g):
            rows = dram[g * XT * NP:(g + 1) * XT * NP, :]
            return rows.rearrange("(t p) d -> p t d", p=NP)

        def tail_rows(dram):
            return dram[NSUP * NB:N, :]

        @block.sync
        def _(sp):
            def load_x(g):
                v = x_view(x, g)
                for a, b in ((0, LO), (LO, NP)):
                    sp.dma_start(x_sb[a:b, g * XT:(g + 1) * XT, :], v[a:b]).then_inc(s_x[g], 16)

            load_x(0)
            load_x(1)
            rows3 = (3 * RC) * P
            whole = E // P - 3 * RC
            left = E - (E // P) * P
            for a, e in enumerate((src, dst)):
                sp.dma_start(edge_i[:, a, 0:3, :],
                             e[0:rows3].rearrange("(t c e) -> c t e", t=3, e=P)).then_inc(s_edges, 16)
                sp.dma_start(edge_i[0:whole, a, 3, :],
                             e[rows3:rows3 + whole * P].rearrange("(c e) -> c e", e=P)).then_inc(s_edges, 16)
            sp.wait_ge(s_pads, 2)
            for a, e in enumerate((src, dst)):
                sp.dma_start(edge_i[whole:whole + 1, a, 3, 0:left],
                             e[E - left:E].rearrange("(c e) -> c e", c=1)).then_inc(s_edges, 16)
            for g in range(2, XG):
                load_x(g)
            for v, e in enumerate((b1, gamma, beta)):
                sp.dma_start(vec_rows[v * KH:(v + 1) * KH, :], e.rearrange("(k p) -> k p", p=P)).then_inc(s_vecs, 16)
            sp.wait_ge(s_zrow, 1)
            sp.dma_start(h_rows[N:N + 1, :], zeros[0:1, 0:ROW]).then_inc(s_zst, 16)
            sp.dma_start(w1[:, :, :], W1.rearrange("(k p) h -> p k h", p=P)).then_inc(s_w1, 16)
            for g in range(XG):
                sp.wait_ge(s_lop, g + 1)
                sp.wait_ge(s_lo, g + 1)
                sp.wait_ge(s_mid, g + 1)
                sp.wait_ge(s_midp, g + 1)
                sp.wait_ge(s_hi, g + 1)
                v = x_view(h_rows, g)
                for a, b in ((0, LO), (LO, NP)):
                    sp.dma_start(v[a:b], hp[a:b, g * XT:(g + 1) * XT, :, :]
                                 .rearrange("p t s d -> p t (s d)")).then_inc(s_hrow, 16)

            def load(row0, b):
                sp.dma_start(x2[:, b, :, :],
                             x[bass.ds(row0, HALF), :].rearrange("(s p) d -> p s d", p=P)).then_inc(s_x2[b], 16)

            def store(row0, b):
                sp.dma_start(out[bass.ds(row0, HALF), :].rearrange("(s p) d -> p s d", p=P),
                             o2[:, b, :, :]).then_inc(s_st[b], 16)

            sp.wait_ge(s_used, 1)
            sp.dma_start(w2[:, :, :], W2.rearrange("(k p) d -> p k d", p=P)).then_inc(s_w2, 16)
            sp.dma_start(b2b[:, :], b2.rearrange("(a d) -> a d", a=1).to_broadcast([P, D])).then_inc(s_b2, 16)
            for b in (0, 1):
                load(b * HALF, b)
            with sp.Fori(0, NSUP - 1) as i:
                for b in (0, 1):
                    sp.wait_ge(s_o2, 2 * i + b + 1)
                    store(i * NB + b * HALF, b)
                    load((i + 1) * NB + b * HALF, b)
            for b in (0, 1):
                sp.wait_ge(s_o2, 2 * (NSUP - 1) + b + 1)
                store((NSUP - 1) * NB + b * HALF, b)
                if b == 0:
                    sp.dma_start(x2[0:REST, 0, 0, :], tail_rows(x)).then_inc(s_x2[0], 16)
            sp.wait_ge(s_o2, 2 * NSUP + 1)
            sp.dma_start(tail_rows(out), o2[0:REST, 0, 0, :]).then_inc(s_st[0], 16)
            sp.wait_ge(s_st[0], 16 * (NSUP + 1))
            sp.wait_ge(s_st[1], 16 * NSUP)

        @block.gpsimd
        def _(pool):
            pool.memset(edge_i[RC - 2:RC, 0, 3, :], N).then_inc(s_pads, 1)
            pool.wait_ge(s_pads, 1)
            pool.memset(edge_i[RC - 2:RC, 1, 3, :], N - 1).then_inc(s_pads, 1)
            pool.wait_ge(s_pads, 2)
            pool.memset(ident[:, :], 0.0).then_inc(s_ident, 1)
            pool.memset(ones[:, :], 1.0).then_inc(s_const, 1)
            pool.memset(epst[:, :], EPS).then_inc(s_const, 1)
            for v, bound in enumerate(LEAST + MOST):
                pool.memset(bounds[:, v:v + 1], float(bound)).then_inc(s_pad, 1)
            loose = dict(channel_multiplier=0, allow_small_or_imprecise_dtypes=True)
            pool.iota(iota_f[:, :], pattern=[[1, P]], base=0, **loose).then_inc(s_const, 1)
            pool.iota(win_f, pattern=[[STEP, G]],
                      base=-SLACK, **loose).then_inc(s_const, 1)
            pool.wait_ge(s_ident, 1)
            pool.affine_select(out=ident[:, :], in_=ident[:, :], compare_op=ALU.not_equal, fill=1.0, base=0,
                               pattern=[[-1, P]], channel_multiplier=1).then_inc(s_ident, 1)
            pool.memset(src_tab[:, C:CX], 0).then_inc(s_pad, 1)
            pool.memset(dst_rel[:, C:CX], 0.0).then_inc(s_pad, 1)
            pool.memset(row0[:, :], 0.0).then_inc(s_row0, 1)
            pool.wait_ge(s_row0, 1)
            pool.memset(row0[0:1, :], 1.0).then_inc(s_row0, 1)
            for i in range(NPAIR):
                pool.iota(blk_f[:, i * GP * CG:(i + 1) * GP * CG], pattern=[[0, GP * CG]],
                          base=i * PAIR + NB, **loose).then_inc(s_pad, 1)
            pool.memset(blk_f[:, NPAIR * GP * CG:C], 0.0).then_inc(s_pad, 1)
            pool.memset(zeros[0:1, 0:ROW].bitcast(I32), 0).then_inc(s_zrow, 1)
            pool.wait_ge(s_edges, 96)
            pool.tensor_copy(edge_f[:, :, :, :], edge_i[:, :, :, :]).then_inc(s_efl, 1)
            pool.memset(hT[:, :, N:HTW], 0.0).then_inc(s_pad, 1)
            pool.iota(iota_k[:, :], pattern=[[1, KEYS]], base=0, **loose).then_inc(s_pad, 1)

            for g in range(XG):
                residue(pool, g, slice(g * XT + SPLIT[g], (g + 1) * XT), slice(SPLIT[g], XT), s_resp, s_lop, s_midp)
            pool.wait_ge(s_zrow, 1)
            pool.wait_ge(s_zst, 16)
            pool.memset(counts[:, :, :].bitcast(I32), 0).then_inc(s_zero, 1)

            pool.wait_ge(s_flag, 1)
            irregular = pool.value_load(flag[0:1, 0:1], min_val=0, max_val=P)
            pool.wait_ge(s_hrow, 16 * 2 * XG)

            def gather(to, index, done):
                pool.indirect_dma_start(to, None, h_rows,
                                        bass.IndirectOffsetOnAxis(ap=index, axis=0)).then_inc(done, 16)

            with pool.If(irregular == 0):
                def group(q, g, first):
                    pool.wait_ge(s_idx, g + 1)
                    if not first:
                        pool.wait_ge(s_win, g - Q + 1)
                    pool.sem_inc(s_turn, 1)
                    for c in range(CG):
                        gather(g_ring[:, q, c, :], idx_ring[:, q, c:c + 1], s_gath[q])

                for q in range(Q):
                    group(q, q, True)
                with pool.Fori(1, NG // Q) as r:
                    for q in range(Q):
                        group(q, r * Q + q, False)
                for g in range(NG // Q * Q, NG):
                    group(g % Q, g, False)
            with pool.Else():
                pool.iota(node_iota.bitcast(I32), pattern=[[1, N]], base=0,
                          channel_multiplier=0).then_inc(s_giota, 1)
                with pool.Fori(0, KD * C) as c:
                    pool.wait_ge(s_gidx, c + 1)
                    pool.sem_inc(s_turn, 1)
                    gather(g_ring[:, 0, 0, :], idx_ring[:, 0, 0:1], s_ggath)

        @block.tensor
        def _(pe):
            pe.wait_ge(s_ident, 2)
            pe.wait_ge(s_efl, 1)
            for a in range(2):
                for t in range(4):
                    last = pe.transpose(p_tab[a][:, t * RC:(t + 1) * RC], edge_f[:, a, t, :], ident[0:RC, 0:RC])
            last.then_inc(s_tabT, 1)
            pe.wait_ge(s_row0, 2)
            pe.wait_ge(s_dtab, 1)
            pe.matmul(p_tab[0][:, :], row0[:, :], dst_tab[:, :], start=True, stop=True).then_inc(s_first, 1)
            pe.wait_ge(s_vecs, 48)
            pe.transpose(ps[:, 7, 0:3 * KH], vec_rows[:, :], ident[0:3 * KH, 0:3 * KH]).then_inc(s_vecT, 1)
            for t in range(NT):
                if t % XT == 0:
                    pe.wait_ge(s_h32, t // XT + 1)
                if t >= TR:
                    pe.wait_ge(s_hTc, t - TR + 1)
                for f in range(KD):
                    last = pe.transpose(p_tr[t % TR][:, f, :], h32[0:NP, t, f * P:(f + 1) * P], ident[0:NP, 0:NP])
                last.then_inc(s_hTp, 1)
                if t == NT - TR - 1:
                    pe.wait_ge(s_viol, 1)
                    pe.matmul(ps[0:1, 6, 0:len(LEAST + MOST)], ones[:, :], broken[:, :],
                              start=True, stop=True).then_inc(s_vsum, 1)

            pe.wait_ge(s_flag, 1)
            irregular = pe.value_load(flag[0:1, 0:1], min_val=0, max_val=P)
            pe.wait_ge(s_w1, 16)

            def hidden(col, n, k, m, fs=range(KD)):
                for f in fs:
                    if f == 0:
                        pe.wait_ge(s_h1, FREE + m - 2)
                    last = pe.matmul(p_hid[k % 2][:, 0:n], w1[:, f, k * P:(k + 1) * P],
                                     hT[:, f, bass.ds(col, n)], start=(f == 0), stop=(f == KD - 1))
                    if f == KD - 1:
                        last.then_inc(s_hid, 1)

            def rest_tiles(k0):
                for k in (k0, k0 + 1):
                    for f in range(KD):
                        last = pe.matmul(p_rest[k], w1[:, f, k * P:(k + 1) * P],
                                         hT[:, f, NSUP * NB:N], start=(f == 0), stop=(f == KD - 1))
                    last.then_inc(s_rhid, 1)

            with pe.If(irregular == 0):
                def group(i, s, lead=False):
                    n, q = i * SLOTS + s, s % Q
                    r = i * (SLOTS // Q) + s // Q
                    pe.wait_ge(s_gath[q], (r + 1) * (16 * CG))
                    pe.wait_ge(s_hot, n + 1)
                    if not lead or s >= 2:
                        pe.wait_ge(s_add, n - 1)
                    for f in range(KD):
                        for c in range(CG):
                            for p in range(PARTS):
                                o = p * D + f * P
                                last = pe.matmul(p_win[q % 2][:, f, :], g_ring[:, q, c, o:o + P],
                                                 d_ring[q][:, c, :], start=(c + p == 0),
                                                 stop=(c == CG - 1 and p == PARTS - 1))
                    last.then_inc(s_win, 1)

                def count(i, k, c, lead):
                    m = i * DC + k * CG + c
                    if c == 0:
                        pe.wait_ge(s_src, i * DB + k + 1)
                        if not lead and k == 0:
                            pe.wait_ge(s_aadd, i)
                    pe.wait_ge(s_key, m + 1)
                    if not lead or k:
                        pe.wait_ge(s_cadd, m - CG + 1)
                    pe.matmul(ps[:, 4 + c, 0:KEYS], src_ring[:, k % 2, c, :], key_ring[:, c, :],
                              start=True, stop=True).then_inc(s_cnt, 1)

                def times_h(i, s):
                    e = s - XS
                    t0, t1 = (NT * x // (SLOTS - XS) for x in (e, e + 1))
                    if e == 0:
                        pe.wait_ge(s_cadd, (i + 1) * DC)
                    for t in range(t0, t1):
                        for p in range(PARTS):
                            for f in range(KD):
                                last = pe.matmul(p_agg[f], hp[:, t, p, f * P:(f + 1) * P], counts[0:NP, t, :],
                                                 start=(t + p == 0), stop=(t == NT - 1 and p == PARTS - 1))
                    last.then_inc(s_agg, 1)

                def hidden_of_pair(i, h, f):
                    if h + f == 0:
                        pe.wait_ge(s_add, (i + 1) * SLOTS)
                    if h == KH and f == 0:
                        pe.wait_ge(s_add, (i + 1) * SLOTS + TAIL)
                        pe.wait_ge(s_aadd, i + 1)
                    hidden(i * PAIR + h // KH * NB, NB, h % KH, i * (2 * KH) + h + 1, (f,))

                def counting_slot(i, s, lead):
                    if s >= 0:
                        group(i, s, lead)
                    for what, a, b in slot_work(s, lead):
                        if what == "count":
                            count(i, a, b, lead)
                        else:
                            hidden_of_pair(i - 1, a, b)

                pe.wait_ge(s_hTc, NT)
                for s in range(-1, XS):
                    counting_slot(0, s, True)
                for s in range(XS, SLOTS):
                    group(0, s)
                    times_h(0, s)
                with pe.Fori(1, NPAIR) as i:
                    for s in range(XS):
                        counting_slot(i, s, False)
                    for s in range(XS, SLOTS):
                        group(i, s)
                        times_h(i, s)
                i = NPAIR - 1
                for h in range(2 * KH):
                    if h in TAIL_AT:
                        group(i, SLOTS + TAIL_AT.index(h))
                    for f in range(KD):
                        hidden_of_pair(i, h, f)
                    if KH <= h < KH + KH // 2:
                        rest_tiles(2 * (h - KH))
            with pe.Else():
                pe.sem_inc(s_gused, 1)
                pe.wait_ge(s_zero, 1)
                for f in range(KD):
                    if f:
                        pe.wait_ge(s_gadd, f)
                    else:
                        pe.wait_ge(s_hTc, NT)
                        pe.wait_ge(s_vec, 1)
                    for b in range(GB):
                        pe.matmul(ps[:, b, :], zcols[:, 0:P], zcols[:, :], start=True, stop=False)
                    with pe.Fori(0, C) as c:
                        pe.wait_ge(s_ggath, 16 * (f * C + c + 1))
                        pe.wait_ge(s_ghot, f * C + c + 1)
                        for s in range(PARTS):
                            o = s * D + f * P
                            for b in range(GB):
                                n = min(NB, N - b * NB)
                                last = pe.matmul(ps[:, b, 0:n], g_ring[:, 0, 0, o:o + P],
                                                 onehot_all[:, b * NB:b * NB + n], start=False, stop=False)
                        last.then_inc(s_gused, 1)
                    for b in range(GB):
                        last = pe.matmul(ps[:, b, :], zcols[:, 0:P], zcols[:, :], start=False, stop=True)
                    last.then_inc(s_gopen, 1)
                pe.wait_ge(s_gadd, KD)
                with pe.Fori(0, NSUP) as J:
                    for k in range(KH):
                        hidden(J * NB, NB, k, J * KH + k + 1)
                for k in range(0, KH, 2):
                    rest_tiles(k)

            pe.wait_ge(s_w2, 16)

            def product(b, k0, half):
                for s in range(2):
                    for k in range(half * KH // 2, (half + 1) * KH // 2):
                        if s == 0:
                            k0 = k0 + 1
                            pe.wait_ge(s_hn, k0)
                        last = pe.matmul(p_out[b][:, s, :], hn[:, b, k, s * P:(s + 1) * P], w2[:, k, :],
                                         start=(k == 0), stop=(k == KH - 1))
                if half == 1:
                    last.then_inc(s_out, 1)

            for half in (0, 1):
                for b in (0, 1):
                    product(b, (2 * half + b) * (KH // 2), half)
            with pe.Fori(1, NSUP) as i:
                for b in (0, 1):
                    pe.wait_ge(s_bias, 2 * i + b - 1)
                    for half in (0, 1):
                        product(b, (2 * i + b) * KH + half * (KH // 2), half)
            pe.wait_ge(s_bias, 2 * NSUP - 1)
            for k in range(KH):
                pe.wait_ge(s_hn, 2 * NSUP * KH + k + 1)
                last = pe.matmul(p_out[0][0:REST, 0, :], hn[:, 0, k, 0:REST], w2[:, k, :],
                                 start=(k == 0), stop=(k == KH - 1))
            last.then_inc(s_out, 1)

        @block.scalar
        def _(act):
            act.wait_ge(s_const, 4)
            act.activation(bstd[:, 0:1], epst[:, :], ACT.Sqrt)

            def middle(g):
                act.wait_ge(s_res, g + 1)
                act.activation(hp[:, g * XT:g * XT + SPLIT[g], 1, :], high(res[:, g % 2, 0:SPLIT[g], :]),
                               ACT.Copy).then_inc(s_mid, 1)

            def deviations(g):
                ts = slice(g * XT, (g + 1) * XT)
                act.wait_ge(s_var, g + 1)
                act.activation(std[:, ts], mv[:, ts, 1], ACT.Sqrt, bias=epst[0:NP, :]).then_inc(s_std, 1)

            deviations(0)
            for g in range(XG):
                ts = slice(g * XT, (g + 1) * XT)
                act.wait_ge(s_norm, g + 1)
                for t in range(g * XT, (g + 1) * XT):
                    last = act.activation(h32[0:NP, t, :], x_sb[0:NP, t, :], ACT.Relu,
                                          bias=nbias[:, t:t + 1], scale=rstd[:, t:t + 1])
                last.then_inc(s_h32, 1)
                if g + 1 < XG:
                    deviations(g + 1)
                act.wait_ge(s_h32, g + 1)
                act.activation(hp[:, ts, 0, :], high(h32[0:NP, ts, :]), ACT.Copy).then_inc(s_hi, 1)
                if g:
                    middle(g - 1)
            middle(XG - 1)

            def indices(q, g):
                act.activation(idx_ring[:, q, :], src_tab[:, bass.ds(g * CG, CG)], ACT.Copy).then_inc(s_idx, 1)

            act.wait_ge(s_dtab, 1)
            for q in range(Q):
                indices(q, q)
            for t in range(NT):
                act.wait_ge(s_hTp, t + 1)
                act.activation(hT[:, :, t * NP:(t + 1) * NP], p_tr[t % TR][:, :, :],
                               ACT.Copy).then_inc(s_hTc, 1)

            act.wait_ge(s_flag, 1)
            irregular = act.value_load(flag[0:1, 0:1], min_val=0, max_val=P)
            act.wait_ge(s_vec, 1)
            act.wait_ge(s_pad, PADS)
            act.sem_inc(s_h1, FREE)

            def store_hidden(col, n, k, m):
                act.wait_ge(s_hid, m + 1 if k == KH - KD else m)
                act.activation(h1[:, k, bass.ds(col, n)], p_hid[k % 2][:, 0:n], ACT.Identity,
                               bias=vec[:, k:k + 1]).then_inc(s_h1, 1)

            def store_rest(k0):
                for k in (k0, k0 + 1):
                    act.wait_ge(s_rhid, k0 + 2)
                    act.activation(h1[:, k, NSUP * NB:N], p_rest[k], ACT.Identity,
                                   bias=vec[:, k:k + 1]).then_inc(s_rh1, 1)

            def bn_deviation(half):
                ks = slice(half * KH // 2, (half + 1) * KH // 2)
                act.wait_ge(s_bvar, half + 1)
                act.activation(bstd[:, ks], bmv[:, ks, 1], ACT.Sqrt, bias=epst[:, :]).then_inc(s_bsd, 1)
                act.wait_ge(s_bn, half + 1)

            def normalise(b, col, n, half):
                for k in range(half * KH // 2, (half + 1) * KH // 2):
                    act.activation(hn[:, b, k, 0:n], h1[:, k, bass.ds(col, n)], ACT.Relu,
                                   bias=bshift[:, k:k + 1], scale=bscale[:, k:k + 1]).then_inc(s_hn, 1)

            with act.If(irregular == 0):
                def refill(i, s):
                    q = s % Q
                    act.wait_ge(s_gath[q], (i * (SLOTS // Q) + s // Q + 1) * (16 * CG))
                    indices(q, i * GP + gathered_group(s + Q))

                def src_onehots(i, k, lead):
                    m = i * DB + k
                    if not lead or k:
                        act.wait_ge(s_src, m)
                    for c in range(CG):
                        at = (i * (GP * CG) + D0 * CG) + k * CG + c
                        last = act.activation(sq[:, c, :], iota_f[:, :], ACT.Square,
                                              bias=neg_rem[:, bass.ds(at, 1)])
                    last.then_inc(s_sq, 1)
                    act.wait_ge(s_sq, m + 1)
                    if not lead or k >= 2:
                        act.wait_ge(s_cnt, (m - 1) * CG)
                    act.activation(src_ring[:, k % 2, :, :], sq[:, :, :], ACT.Relu, bias=1.0,
                                   scale=-1.0).then_inc(s_src, 1)

                def store_tiles(i, h):
                    for g in ([h - 1, h] if h % KH == KH - 1 else [h] if h % KH < KH - 2 else []):
                        store_hidden(i * PAIR + g // KH * NB, NB, g % KH, i * (2 * KH) + g + 1)

                def counting_slot(i, s, lead):
                    if s >= 0:
                        refill(i, s)
                    for what, a, b in slot_work(s, lead):
                        if what == "count" and b == 0 and a + 1 < DB:
                            src_onehots(i, a + 1, lead)
                        if what == "hidden" and b == KD - 1:
                            store_tiles(i - 1, a)

                act.wait_ge(s_viol, 1)
                act.wait_ge(s_lo, XG)
                act.wait_ge(s_lop, XG)
                src_onehots(0, 0, True)
                for s in range(-1, XS):
                    counting_slot(0, s, True)
                for s in range(XS, SLOTS):
                    refill(0, s)
                with act.Fori(1, NPAIR) as i:
                    src_onehots(i, 0, False)
                    for s in range(XS):
                        counting_slot(i, s, False)
                    for s in range(XS, SLOTS):
                        refill(i, s)
                i = NPAIR - 1
                for h in range(2 * KH):
                    store_tiles(i, h)
                    if KH <= h < KH + KH // 2:
                        store_rest(2 * (h - KH))
                    if h == KH + KH // 2 - 1:
                        bn_deviation(0)
                    if h - KH - KH // 2 in (0, 1):
                        b = h - KH - KH // 2
                        normalise(b, b * HALF, HALF, 0)
            with act.Else():
                with act.Fori(0, NSUP) as J:
                    for k in range(KH):
                        store_hidden(J * NB, NB, k, J * KH + k + 1)
                for k in range(0, KH, 2):
                    store_rest(k)
                bn_deviation(0)
                for b in (0, 1):
                    normalise(b, b * HALF, HALF, 0)
            bn_deviation(1)
            for b in (0, 1):
                normalise(b, b * HALF, HALF, 1)
            with act.Fori(1, NSUP) as i:
                for b in (0, 1):
                    act.wait_ge(s_out, 2 * i + b - 1)
                    for half in (0, 1):
                        normalise(b, i * NB + b * HALF, HALF, half)
            act.wait_ge(s_out, 2 * NSUP - 1)
            for half in (0, 1):
                normalise(0, NSUP * NB, REST, half)

        @block.vector
        def _(dve):
            step = [0]

            def chain(ins):
                step[0] += 1
                ins.then_inc(s_dve, 1)
                dve.wait_ge(s_dve, step[0])

            def layer_stats(g):
                dve.wait_ge(s_x[g], 32)
                for t in range(g * XT, (g + 1) * XT):
                    last = dve.bn_stats(stats[:, t, :], x_sb[0:NP, t, :])
                chain(last)
                for t in range(g * XT, (g + 1) * XT):
                    last = dve.bn_aggr(mv[:, t, :], stats[:, t, :])
                last.then_inc(s_var, 1)

            def layer_parts(g):
                ts = slice(g * XT, (g + 1) * XT)
                dve.wait_ge(s_std, g + 1)
                chain(dve.reciprocal(rstd[:, ts], std[:, ts]))
                dve.scalar_tensor_tensor(nbias[:, ts], mv[:, ts, 0], -1.0, rstd[:, ts],
                                         ALU.mult, ALU.mult).then_inc(s_norm, 1)

            def layer_residue(g):
                residue(dve, g, slice(g * XT, g * XT + SPLIT[g]), slice(0, SPLIT[g]), s_res, s_lo)

            def edge_tables():
                dve.wait_ge(s_tabT, 1)
                dve.tensor_copy(src_tab[:, 0:C], p_tab[0][:, :])
                dve.tensor_scalar(quot[:, :], p_tab[0][:, :], 1.0 / NP, -(NP // 2) / NP, ALU.mult, ALU.add)
                dve.tensor_copy(neg_rem[:, :], p_tab[0][:, :])
                dve.tensor_copy(dst_tab[:, :], p_tab[1][:, :]).then_inc(s_dtab, 1)

            counted = slice(D0 * CG, D1 * CG)

            def counted_part(t):
                return t[:, 0:NPAIR * GP * CG].rearrange("p (i c) -> p i c", i=NPAIR)[:, :, counted]

            span, where = counted_part(key), counted_part(pos_f)

            def tables_relative():
                dve.wait_ge(s_const, 4)
                dve.wait_ge(s_pad, NPAIR + 11)
                dve.wait_ge(s_first, 1)
                first = p_tab[0]
                chain(dve.tensor_scalar(quot[:, :], quot[:, :], MAGIC, MAGIC, ALU.add, ALU.subtract))
                by_group = first.rearrange("p (g c) -> p g c", c=CG)[:, :, 0]
                dve.tensor_tensor(dst_rel[:, 0:C].rearrange("p (g c) -> p g c", c=CG),
                                  dst_tab.rearrange("p (g c) -> p g c", c=CG),
                                  by_group.unsqueeze(2).to_broadcast([P, G, CG]), ALU.subtract)
                dve.tensor_copy(start[:, :], by_group[0:1])
                dve.tensor_tensor(early[:, :], by_group, win_f, ALU.subtract)
                dve.tensor_tensor(key[:, :], dst_tab[:, :], first[:, :], ALU.subtract)
                dve.tensor_tensor(pos_f[:, :], first[:, :], blk_f, ALU.subtract)
                chain(dve.scalar_tensor_tensor(neg_rem[:, :], quot[:, :], float(NP), neg_rem[:, :],
                                               ALU.mult, ALU.subtract))
                dve.tensor_copy(pos[:, :], pos_f[0:1, :])
                steps = where.shape[2] - DEG
                chain(dve.tensor_tensor(grow[:, :, :], where[:, :, DEG:], where[:, :, 0:steps], ALU.subtract))

            def tables_checked():
                n = len(LEAST)
                values = ((dst_rel[:, 0:C], AX.X), (span, AX.XY), (where, AX.XY), (grow[:, :, :], AX.XY),
                          (early[:, :], AX.X))
                for v, (t, axis) in enumerate(values):
                    last = dve.tensor_reduce(found[:, v:v + 1], t, axis, ALU.min)
                    if v < len(MOST):
                        dve.tensor_reduce(found[:, n + v:n + v + 1], t, axis, ALU.max)
                chain(last)
                dve.tensor_tensor(broken[:, 0:n], found[:, 0:n], bounds[:, 0:n], ALU.is_lt)
                dve.tensor_tensor(broken[:, n:], found[:, n:], bounds[:, n:], ALU.is_gt).then_inc(s_viol, 1)
                chain(dve.scalar_tensor_tensor(key[:, :], quot[:, :], float(DW), key[:, :], ALU.mult, ALU.add))

            layer_stats(0)
            layer_parts(0)
            layer_stats(1)
            layer_parts(1)
            layer_stats(2)
            for g in range(2, XG):
                if g + 1 < XG:
                    layer_stats(g + 1)
                else:
                    edge_tables()
                layer_parts(g)
                layer_residue(g - 2)
            layer_residue(XG - 2)
            layer_residue(XG - 1)
            tables_relative()
            dve.wait_ge(s_vecT, 1)
            dve.tensor_copy(vec[:, :], ps[:, 7, 0:3 * KH]).then_inc(s_vec, 1)
            tables_checked()
            dve.wait_ge(s_vsum, 1)
            dve.tensor_reduce(flag[:, :], ps[0:1, 6, 0:len(LEAST + MOST)], AX.X, ALU.max).then_inc(s_flag, 1)

            dve.wait_ge(s_flag, 1)
            irregular = dve.value_load(flag[0:1, 0:1], min_val=0, max_val=P)
            dve.wait_ge(s_pad, PADS)

            bst_v = bst[:, :, :, :].rearrange("p k j s -> p k (j s)")

            def hidden_stats_at(J, k, m):
                dve.wait_ge(s_h1, FREE + m)
                dve.bn_stats(bst_v[:, k, bass.ds(J * 6, 6)], h1[:, k, bass.ds(J * NB, NB)]).then_inc(s_bst, 1)

            def rest_stats(k0):
                for k in (k0, k0 + 1):
                    dve.wait_ge(s_rh1, k + 1)
                    dve.bn_stats(bst[:, k, NSUP, :], h1[:, k, NSUP * NB:N]).then_inc(s_bst, 1)

            def batch_norm(half, stats_done):
                a, b = half * KH // 2, (half + 1) * KH // 2
                dve.wait_ge(s_bst, stats_done)
                for k in range(a, b):
                    last = dve.bn_aggr(bmv[:, k, :], bst[:, k, :, :])
                last.then_inc(s_bvar, 1)
                dve.wait_ge(s_bsd, half + 1)
                chain(dve.reciprocal(brstd[:, a:b], bstd[:, a:b]))
                chain(dve.tensor_tensor(bscale[:, a:b], brstd[:, a:b], vec[:, KH + a:KH + b], ALU.mult))
                chain(dve.tensor_tensor(bms[:, a:b], bmv[:, a:b, 0], bscale[:, a:b], ALU.mult))
                dve.tensor_tensor(bshift[:, a:b], vec[:, 2 * KH + a:2 * KH + b], bms[:, a:b],
                                  ALU.subtract).then_inc(s_bn, 1)

            before_branch = step[0]

            with dve.If(irregular == 0):
                iota_b = iota_f[:, 0:W].unsqueeze(1).to_broadcast([P, CG, W])

                def onehots(q, g):
                    rel = dst_rel[:, bass.ds(g * CG, CG)].unsqueeze(2).to_broadcast([P, CG, W])
                    dve.tensor_tensor(d_ring[q], iota_b, rel, ALU.is_equal).then_inc(s_hot, 1)

                def window(i, s, last, lead=False):
                    n, q = i * SLOTS + s, s % Q
                    at = window_start(i, s)
                    if not lead or s:
                        dve.wait_ge(s_add, n)
                    if s % SLOTS < TAIL and not lead:
                        dve.wait_ge(s_aadd, i + s // SLOTS)
                    dve.wait_ge(s_win, n + 1)
                    w = hT[:, :, bass.ds(at, W)]
                    dve.tensor_tensor(w, w, p_win[q % 2][:, :, :], ALU.add).then_inc(s_add, 1)
                    if not last:
                        onehots(q, i * GP + gathered_group(s + Q))

                starts = []

                def window_start(i, s):
                    runs = (0, XS), (XS, D0), (D0, SLOTS), (SLOTS, SLOTS + TAIL)
                    a, b = next(r for r in runs if s < r[1])
                    if s == a:
                        _, starts[:] = nc.values_load_multi_w_load_instructions(
                            start[0:1, bass.ds(i * GP + gathered_group(a), b - a)], engines=[dve.engine],
                            min_val=0, max_val=N, skip_runtime_bounds_check_because="dst is a node")
                    return starts[s - a]

                def count_step(i, k, c, lead):
                    m = i * DC + k * CG + c
                    if k:
                        add_counts(m - CG, c, added_at(i, k - 1, c), lead and k == 1 and c == 0)
                    if k < DB:
                        at = (i * (GP * CG) + D0 * CG) + k * CG + c
                        dve.tensor_scalar(key_ring[:, c, :], iota_k[:, :], key[:, bass.ds(at, 1)], None,
                                          ALU.is_equal).then_inc(s_key, 1)

                positions = []

                def added_at(i, k, c):
                    if k % LB == 0 and c == 0:
                        at = (i * (GP * CG) + D0 * CG) + k * CG
                        _, positions[:] = nc.values_load_multi_w_load_instructions(
                            pos[0:1, bass.ds(at, LB * CG)], engines=[dve.engine], min_val=0, max_val=NB - DW,
                            skip_runtime_bounds_check_because="the regular path has checked them")
                    return positions[k % LB * CG + c]

                def counting_slot(i, s, lead):
                    work = [(k, c) for k in count_batches(s, lead) for c in range(CG)]
                    for j, (k, c) in enumerate(work):
                        if j == len(work) // 2 and s >= 0:
                            window(i, s, False, lead)
                        count_step(i, k, c, lead)
                    if s == XS - 1:
                        for c in range(CG):
                            count_step(i, DB, c, lead)

                def add_counts(m, c, where, first):
                    if not first:
                        dve.wait_ge(s_cadd, m)
                    dve.wait_ge(s_cnt, m + 1)
                    a = counts[:, :, bass.ds(where, DW)]
                    dve.tensor_tensor(a, a, p_cnt[c], ALU.add).then_inc(s_cadd, 1)

                def add_block(i):
                    dve.wait_ge(s_agg, (i + 1) * (SLOTS - XS))
                    dve.wait_ge(s_add, (i + 1) * SLOTS)
                    b = hT[:, :, bass.ds(i * PAIR + NB, NB)]
                    dve.tensor_tensor(b, b, ps[:, 6:8, :], ALU.add).then_inc(s_aadd, 1)

                def zero_counts(i, s):
                    e = s - XS
                    t0, t1 = (NT * x // (SLOTS - XS) for x in (e, e + 1))
                    dve.wait_ge(s_agg, i * (SLOTS - XS) + e + 1)
                    dve.memset(counts[:, t0:t1, :].bitcast(I32), 0).then_inc(s_zero, 1)

                def stats_of(i, h):
                    hidden_stats_at(i * 2 + h // KH, h % KH, i * (2 * KH) + h + 1)

                for q in range(Q):
                    onehots(q, gathered_group(q))
                dve.wait_ge(s_zero, 1)
                dve.wait_ge(s_hTc, NT)
                def product_slot(i, s, lead):
                    window(i, s, False, lead)
                    if s == SLOTS - 1:
                        add_block(i)
                    zero_counts(i, s)
                    if not lead:
                        e, n = s - XS, SLOTS - XS - 1
                        for h in range(2 * KH * e // n, min(2 * KH, 2 * KH * (e + 1) // n)):
                            stats_of(i - 1, h)

                for s in range(-1, XS):
                    counting_slot(0, s, True)
                for s in range(XS, SLOTS):
                    product_slot(0, s, True)
                with dve.Fori(1, NPAIR) as i:
                    dve.wait_ge(s_zero, i * (SLOTS - XS) + 1)
                    for s in range(XS):
                        counting_slot(i, s, False)
                    for s in range(XS, SLOTS):
                        product_slot(i, s, False)
                i = NPAIR - 1
                dve.wait_ge(s_zero, NPAIR * (SLOTS - XS) + 1)
                dve.sem_inc(s_used, 1)
                for h in range(2 * KH):
                    if h in TAIL_AT:
                        window(i, SLOTS + TAIL_AT.index(h), True)
                    stats_of(i, h)
                    if KH <= h < KH + KH // 2:
                        rest_stats(2 * (h - KH))
                    if h == KH + KH // 2 - 1:
                        batch_norm(0, NSUP * KH + KH // 2)
            with dve.Else():
                step[0] = before_branch
                dve.wait_ge(s_giota, 1)
                dve.wait_ge(s_idx, Q)
                dve.tensor_copy(node_iota, node_iota.bitcast(I32)).then_inc(s_giota, 1)
                dve.wait_ge(s_giota, 2)
                for f in range(KD):
                    with dve.Fori(0, C) as c:
                        dve.wait_ge(s_gused, f * C + c + 1)
                        dve.tensor_copy(idx_ring[:, 0, 0:1], src_tab[:, bass.ds(c, 1)]).then_inc(s_gidx, 1)
                        dve.tensor_tensor(onehot_all, node_iota,
                                          dst_tab[:, bass.ds(c, 1)].to_broadcast([P, N]),
                                          ALU.is_equal).then_inc(s_ghot, 1)
                    dve.wait_ge(s_gopen, f + 1)
                    if f == KD - 1:
                        dve.sem_inc(s_used, 1)
                    w = hT[:, f, 0:N]
                    dve.wait_ge(s_hTc, NT)
                    for b in range(GB):
                        n = min(NB, N - b * NB)
                        wb = hT[:, f, b * NB:b * NB + n]
                        last = dve.tensor_tensor(wb, wb, ps[:, b, 0:n], ALU.add)
                    last.then_inc(s_gadd, 1)
                with dve.Fori(0, NSUP) as J:
                    for k in range(KH):
                        hidden_stats_at(J, k, J * KH + k + 1)
                for k in range(0, KH, 2):
                    rest_stats(k)
                batch_norm(0, (NSUP + 1) * KH)
            batch_norm(1, (NSUP + 1) * KH)
            dve.wait_ge(s_b2, 16)
            b2v = b2b[:, :].unsqueeze(1).to_broadcast([P, 2, D])

            def finish(b, m, r, first):
                dve.wait_ge(s_out, m)
                if not first:
                    dve.wait_ge(s_st[b], 16 * r)
                dve.tensor_tensor(o2[:, b, :, :], p_out[b][:, :, :], b2v, ALU.add).then_inc(s_bias, 1)
                dve.wait_ge(s_bias, m)
                dve.wait_ge(s_x2[b], 16 * (r + 1))
                dve.scalar_tensor_tensor(o2[:, b, :, :], o2[:, b, :, :], 0.0, x2[:, b, :, :],
                                         ALU.max, ALU.add).then_inc(s_o2, 1)

            for b in (0, 1):
                finish(b, b + 1, 0, True)
            with dve.Fori(1, NSUP) as i:
                for b in (0, 1):
                    finish(b, 2 * i + b + 1, i, False)
            m = 2 * NSUP + 1
            dve.wait_ge(s_out, m)
            dve.wait_ge(s_st[0], 16 * NSUP)
            dve.tensor_tensor(o2[0:REST, 0, 0, :], p_out[0][0:REST, 0, :], b2b[0:REST, :], ALU.add).then_inc(s_bias, 1)
            dve.wait_ge(s_bias, m)
            dve.wait_ge(s_x2[0], 16 * (NSUP + 1))
            dve.scalar_tensor_tensor(o2[0:REST, 0, 0, :], o2[0:REST, 0, 0, :], 0.0, x2[0:REST, 0, 0, :],
                                     ALU.max, ALU.add).then_inc(s_o2, 1)


_INS = ["x", "src", "dst", "L0_gnn_W1", "L0_gnn_b1", "L0_gnn_gamma", "L0_gnn_beta", "L0_gnn_W2", "L0_gnn_b2"]


def kernel(**inputs):
    import numpy as _np
    import concourse.bacc as _bacc
    from concourse import mybir as _mybir
    from concourse.bass_utils import run_bass_kernel_spmd as _run

    nc = _bacc.Bacc("TRN2", target_bir_lowering=False, num_devices=1)
    arrays, args = {}, []
    for name in _INS:
        a = _np.ascontiguousarray(inputs[name])
        arrays[f"in_{name}"] = a
        args.append(nc.dram_tensor(f"in_{name}", a.shape, _mybir.dt.from_np(a.dtype), kind="ExternalInput").ap())
    args.append(nc.dram_tensor("out_0", (N, D), F32, kind="ExternalOutput").ap())
    build(nc, *args)
    r = _run(nc, [arrays], core_ids=[0])
    return r.results[0]["out_0"]
```
